# Optimizing a Trainium2 kernel written in Bass

```python
import numpy as np
import jax
import jax.numpy as jnp

def _softmax(x, axis=-1):
    return jax.nn.softmax(x, axis=axis)

def _gelu(x):
    return jax.nn.gelu(x, approximate=True)

def _silu(x):
    return jax.nn.silu(x)

def _sigmoid(x):
    return jax.nn.sigmoid(x)

def _layernorm(x, axis=-1, eps=1e-05):
    m = jnp.mean(x, axis=axis, keepdims=True)
    v = jnp.var(x, axis=axis, keepdims=True)
    return (x - m) / jnp.sqrt(v + eps)

def _scatter_add(tgt, idx, src, axis=0):
    return tgt.at[idx].add(src)

def _segment_sum(src, seg, n):
    return jax.ops.segment_sum(src, seg, n)
kernel_name = 'mk_flamingo_gated_d1_seqx_r4_7b5037'

def setup_inputs(seed: int=0):
    np.random.seed(seed)
    _w = jnp.asarray

    def _rec_inputs():
        import jax
        import jax.numpy as jnp
        _rk = jax.random.key(seed)
        x = -0.0002928 + 1 * jax.random.normal(jax.random.fold_in(_rk, 1), (8, 512, 256), jnp.float32)
        _lenS = 512 - jax.random.randint(jax.random.fold_in(_rk, 7), (8,), 0, max(1, 512 // 4) + 1, jnp.int32)
        _lenS2 = 512 - jax.random.randint(jax.random.fold_in(_rk, 8), (8,), 0, max(1, 512 // 4) + 1, jnp.int32)
        _ctx_1024P = jax.random.normal(jax.random.fold_in(_rk, 11), (8, 16, 256), jnp.float32)
        _ctx_1024c = jax.random.dirichlet(jax.random.fold_in(_rk, 511), 0.3 * jnp.ones((16,), jnp.float32), (8, 512))
        _ctx_1024t = jnp.einsum('bsk,bkd->bsd', _ctx_1024c, _ctx_1024P)
        _ctx_1024t = _ctx_1024t * jax.lax.rsqrt(jnp.mean(jnp.square(_ctx_1024t)) + 1e-12) * 0.953939
        ctx_1024 = -1.39393e-06 + 0.999914 * (_ctx_1024t + 0.3 * jax.random.normal(jax.random.fold_in(_rk, 611), (8, 512, 256), jnp.float32))
        _g = jax.random.normal(jax.random.fold_in(_rk, 9001), (2, 1), jnp.float32)
        _g = jnp.sign(_g) * jnp.maximum(jnp.abs(_g), 1.0) + (_g == 0) * 1.0
        g_xattn = _g[0]
        g_ffn = _g[1]
        return (x, ctx_1024, g_xattn, g_ffn)
    x, ctx_1024, g_xattn, g_ffn = _rec_inputs()

    def _L0_xattn_setup():
        import jax, jax.numpy as jnp
        import numpy as np
        import math
        HIDDEN = 256
        HEADS = 16
        HEAD = HIDDEN // HEADS
        SCALE_BASE = 512.0

        def _gammas(heads):
            return 1.0 - jnp.exp(jnp.linspace(math.log(1.0 / 32.0), math.log(1.0 / 512.0), heads))

        def _xpos(x, downscale):
            S, d = (x.shape[2], x.shape[3])
            half = d // 2
            base_scale = (jnp.arange(0, d, 2, dtype=jnp.float32) + 0.4 * d) / (1.4 * d)
            pos = jnp.arange(S, dtype=jnp.float32)
            scale = base_scale[None, :] ** (pos / SCALE_BASE)[:, None]
            if downscale:
                scale = 1.0 / scale
            inv_freq = 1.0 / 10000.0 ** (jnp.arange(half, dtype=jnp.float32) / half)
            sinusoid = pos[:, None] * inv_freq[None, :]
            sin = jnp.repeat(jnp.sin(sinusoid) * scale, 2, axis=-1)
            cos = jnp.repeat(jnp.cos(sinusoid) * scale, 2, axis=-1)
            x1 = x[..., ::2]
            x2 = x[..., 1::2]
            rot = jnp.stack([-x2, x1], axis=-1).reshape(x.shape)
            return x * cos + rot * sin

        def _decay_mask(S, gammas):
            n = jnp.arange(S)[:, None]
            m = jnp.arange(S)[None, :]
            diff = (n - m).astype(jnp.float32)
            mask = n >= m
            pw = jnp.maximum(diff, 0.0)[None, :, :]
            return jnp.where(mask[None, :, :], gammas[:, None, None] ** pw, 0.0)

        def retention_forward(Q, K, V):
            B, S, _ = Q.shape

            def split(x, hd):
                return x.reshape(B, S, HEADS, hd).transpose(0, 2, 1, 3)
            q = _xpos(split(Q, HEAD), downscale=False)
            k = _xpos(split(K, HEAD), downscale=True)
            v = split(V, HEAD)
            D = _decay_mask(S, _gammas(HEADS).astype(Q.dtype))
            scores = jnp.einsum('bhsd,bhtd->bhst', q, k) * D[None]
            out = jnp.einsum('bhst,bhtd->bhsd', scores, v)
            return out.transpose(0, 2, 1, 3).reshape(B, S, HEADS * HEAD)
        key = jax.random.key(seed)
        kq, kk, kv = jax.random.split(key, 3)
        B, S = (2, 512)
        return {'Q': jax.random.normal(kq, (B, S, HIDDEN), dtype=jnp.float32), 'K': jax.random.normal(kk, (B, S, HIDDEN), dtype=jnp.float32), 'V': jax.random.normal(kv, (B, S, HIDDEN), dtype=jnp.float32)}
    _L0_xattn_all = _L0_xattn_setup()
    _L0_xattn_in = {k: v for k, v in _L0_xattn_all.items() if k in ()}
    del _L0_xattn_all

    def _L0_ffn_setup():
        import jax, jax.numpy as jnp
        import numpy as np
        GROUP = 16
        EPS = 1e-05

        def _dequant(q, scale):
            w = q.astype(jnp.float32) / 7.5 - 1.0
            return w * jnp.repeat(scale, GROUP, axis=1)

        def _qlora_linear(x, q, scale, bias, la, lb):
            w = _dequant(q, scale)
            base = jnp.einsum('btd,od->bto', x, w) + bias
            lora = jnp.einsum('btr,or->bto', jnp.einsum('btd,rd->btr', x, la), lb)
            return base + lora

        def _layernorm(x, g, b):
            mu = jnp.mean(x, axis=-1, keepdims=True)
            var = jnp.mean(jnp.square(x - mu), axis=-1, keepdims=True)
            return (x - mu) * jax.lax.rsqrt(var + EPS) * g + b
        key = jax.random.key(seed)
        ks = jax.random.split(key, 6)
        D, R, B, T = (256, 32, 8, 1024)
        x = jax.random.normal(ks[0], (B, T, D), dtype=jnp.float32)
        qweights = jax.random.randint(ks[1], (6, D, D), 0, 16, dtype=jnp.int32)
        scales = jax.random.uniform(ks[2], (6, D, D // GROUP), dtype=jnp.float32)
        biases = jax.random.normal(ks[3], (6, D), dtype=jnp.float32) * 0.02
        lora_a = jax.random.normal(ks[4], (6, R, D), dtype=jnp.float32) * 0.02
        lora_b = jax.random.normal(ks[5], (6, D, R), dtype=jnp.float32) * 0.02
        ln_gamma = jnp.ones((3, D), dtype=jnp.float32)
        ln_beta = jnp.zeros((3, D), dtype=jnp.float32)
        return {'x': x, 'qweights': qweights, 'scales': scales, 'biases': biases, 'lora_a': lora_a, 'lora_b': lora_b, 'ln_gamma': ln_gamma, 'ln_beta': ln_beta}
    _L0_ffn_all = _L0_ffn_setup()
    _L0_ffn_in = {k: v for k, v in _L0_ffn_all.items() if k in ('qweights', 'scales', 'biases', 'lora_a', 'lora_b', 'ln_gamma', 'ln_beta')}
    del _L0_ffn_all
    return {'x': x, 'ctx_1024': ctx_1024, 'g_xattn': g_xattn, 'g_ffn': g_ffn, 'L0_ffn_qweights': _L0_ffn_in['qweights'], 'L0_ffn_scales': _L0_ffn_in['scales'], 'L0_ffn_biases': _L0_ffn_in['biases'], 'L0_ffn_lora_a': _L0_ffn_in['lora_a'], 'L0_ffn_lora_b': _L0_ffn_in['lora_b'], 'L0_ffn_ln_gamma': _L0_ffn_in['ln_gamma'], 'L0_ffn_ln_beta': _L0_ffn_in['ln_beta']}

def reference(x, ctx_1024, g_xattn, g_ffn, L0_ffn_qweights, L0_ffn_scales, L0_ffn_biases, L0_ffn_lora_a, L0_ffn_lora_b, L0_ffn_ln_gamma, L0_ffn_ln_beta):
    import jax
    import jax.numpy as jnp

    def _L0_xattn_ref(Q, K, V):
        import jax, jax.numpy as jnp
        import numpy as np
        import math
        HIDDEN = 256
        HEADS = 16
        HEAD = HIDDEN // HEADS
        SCALE_BASE = 512.0

        def _gammas(heads):
            return 1.0 - jnp.exp(jnp.linspace(math.log(1.0 / 32.0), math.log(1.0 / 512.0), heads))

        def _xpos(x, downscale):
            S, d = (x.shape[2], x.shape[3])
            half = d // 2
            base_scale = (jnp.arange(0, d, 2, dtype=jnp.float32) + 0.4 * d) / (1.4 * d)
            pos = jnp.arange(S, dtype=jnp.float32)
            scale = base_scale[None, :] ** (pos / SCALE_BASE)[:, None]
            if downscale:
                scale = 1.0 / scale
            inv_freq = 1.0 / 10000.0 ** (jnp.arange(half, dtype=jnp.float32) / half)
            sinusoid = pos[:, None] * inv_freq[None, :]
            sin = jnp.repeat(jnp.sin(sinusoid) * scale, 2, axis=-1)
            cos = jnp.repeat(jnp.cos(sinusoid) * scale, 2, axis=-1)
            x1 = x[..., ::2]
            x2 = x[..., 1::2]
            rot = jnp.stack([-x2, x1], axis=-1).reshape(x.shape)
            return x * cos + rot * sin

        def _decay_mask(S, gammas):
            n = jnp.arange(S)[:, None]
            m = jnp.arange(S)[None, :]
            diff = (n - m).astype(jnp.float32)
            mask = n >= m
            pw = jnp.maximum(diff, 0.0)[None, :, :]
            return jnp.where(mask[None, :, :], gammas[:, None, None] ** pw, 0.0)

        def retention_forward(Q, K, V):
            B, S, _ = Q.shape

            def split(x, hd):
                return x.reshape(B, S, HEADS, hd).transpose(0, 2, 1, 3)
            q = _xpos(split(Q, HEAD), downscale=False)
            k = _xpos(split(K, HEAD), downscale=True)
            v = split(V, HEAD)
            D = _decay_mask(S, _gammas(HEADS).astype(Q.dtype))
            scores = jnp.einsum('bhsd,bhtd->bhst', q, k) * D[None]
            out = jnp.einsum('bhst,bhtd->bhsd', scores, v)
            return out.transpose(0, 2, 1, 3).reshape(B, S, HEADS * HEAD)
        return retention_forward(Q, K, V)

    def _L0_ffn_ref(x, qweights, scales, biases, lora_a, lora_b, ln_gamma, ln_beta):
        import jax, jax.numpy as jnp
        import numpy as np
        GROUP = 16
        EPS = 1e-05

        def _dequant(q, scale):
            w = q.astype(jnp.float32) / 7.5 - 1.0
            return w * jnp.repeat(scale, GROUP, axis=1)

        def _qlora_linear(x, q, scale, bias, la, lb):
            w = _dequant(q, scale)
            base = jnp.einsum('btd,od->bto', x, w) + bias
            lora = jnp.einsum('btr,or->bto', jnp.einsum('btd,rd->btr', x, la), lb)
            return base + lora

        def _layernorm(x, g, b):
            mu = jnp.mean(x, axis=-1, keepdims=True)
            var = jnp.mean(jnp.square(x - mu), axis=-1, keepdims=True)
            return (x - mu) * jax.lax.rsqrt(var + EPS) * g + b
        h = x
        for blk in range(3):
            i0, i1 = (2 * blk, 2 * blk + 1)
            y = _qlora_linear(h, qweights[i0], scales[i0], biases[i0], lora_a[i0], lora_b[i0])
            y = _layernorm(y, ln_gamma[blk], ln_beta[blk])
            y = jax.nn.gelu(y, approximate=False)
            y = _qlora_linear(y, qweights[i1], scales[i1], biases[i1], lora_a[i1], lora_b[i1])
            h = y + h
        return h
    x = x + jnp.tanh(g_xattn[0]) * _L0_xattn_ref(_layernorm(x, axis=-1), ctx_1024, ctx_1024)
    x = x + jnp.tanh(g_ffn[0]) * _L0_ffn_ref(_layernorm(x, axis=-1), L0_ffn_qweights, L0_ffn_scales, L0_ffn_biases, L0_ffn_lora_a, L0_ffn_lora_b, L0_ffn_ln_gamma, L0_ffn_ln_beta)
    return x

_drawn_inputs = setup_inputs


def setup_inputs(seed=0):
    import zlib

    import numpy as np

    out = dict(_drawn_inputs(seed))
    spreads = {'L0_ffn_ln_gamma': (1.0, 0.6), 'L0_ffn_ln_beta': (0.0, 0.8)}
    factors = {'L0_ffn_biases': 64.0, 'L0_ffn_lora_a': 8.0, 'L0_ffn_lora_b': 8.0}
    for name, (base, spread) in spreads.items():
        noise = np.random.default_rng([zlib.crc32(name.encode()), seed]).standard_normal(out[name].shape)
        drawn = base * np.exp(spread * noise) if base else spread * noise
        out[name] = jnp.asarray(drawn.astype(out[name].dtype))
    for name, factor in factors.items():
        out[name] = (out[name] * factor).astype(out[name].dtype)
    return out
```

```python
from contextlib import ExitStack

import numpy as np

import concourse.bass as bass
from concourse import mybir
from concourse.alu_op_type import AluOpType as ALU

F32 = mybir.dt.float32
BF16 = mybir.dt.bfloat16
I32 = mybir.dt.int32
ACT = mybir.ActivationFunctionType

B, S, D = 8, 512, 256
HEADS, HD = 16, 16
P = 128
T = S // P
NF = D // P
C = 64
NC = P // C
HH = HEADS // NF
SLOTS = 2
PAIRS = B // SLOTS
UNITS = SLOTS * T
BLOCKS = 3
LAYERS = 2 * BLOCKS
RANK = 32
GROUP = 16
LN_EPS = 1e-5
LN_PASSES = BLOCKS + 1

C_ID, C_DIAG, C_PICK, C_CAUSAL, C_END = 0, P, 2 * P, 3 * P, 3 * P + C


def build(nc, x_d, ctx_d, gates_d, q_d, scale_d, bias_d, la_d, lbt_d, vec_d, const_d, tab_d, out_d):
    es = ExitStack()
    with es:
        def sb(name, shape, dt=F32):
            return es.enter_context(nc.sbuf_tensor(name, shape, dt))

        def sem(name):
            return es.enter_context(nc.semaphore(name))

        def per_slot(name):
            return [sem(f"{name}{s}") for s in range(SLOTS)]

        const = sb("const", [P, C_END])
        ident = const[:, C_ID:C_ID + P]
        diag16 = const[:, C_DIAG:C_DIAG + P]
        pick = const[:, C_PICK:C_PICK + P].rearrange("p (c n) -> p c n", c=NC)
        causal = const[:, C_CAUSAL:C_CAUSAL + C]
        tab = sb("tab", [P, T, 4, D])
        vec = sb("vec", [P, 3, BLOCKS, NF])
        gate = sb("gate", [P, 2])
        tanh_gate = sb("tanh_gate", [P, 2])
        minus_half = sb("minus_half", [P, T])
        wt = sb("wt", [P, LAYERS, NF, D])
        ones = sb("ones", [P, P], BF16)
        bias_h = sb("bias_h", [P, BLOCKS, D], BF16)
        bias_rows = sb("bias_rows", [P, BLOCKS, D], BF16)
        x = sb("x", [P, SLOTS, T, D])
        ctx = sb("ctx", [P, SLOTS, T, D])
        v_chunk = sb("v_chunk", [P, SLOTS, T, HEADS, NC, HD])
        qr = sb("qr", [P, SLOTS, T, D])
        kr = sb("kr", [P, SLOTS, T, D])
        q_prod = sb("q_prod", [P, 2, 2, D])
        k_prod = sb("k_prod", [P, 2, 2, D])
        qT = sb("qT", [P, SLOTS, NF, S])
        kT = sb("kT", [P, SLOTS, NF, S])
        q_wide = sb("q_wide", [P, SLOTS, NF, HH, S])
        sT = sb("sT", [P, 2, HH, C])
        intra = sb("intra", [P, 2, HEADS // 4, C])
        state = sb("state", [P, SLOTS, 4, NF, P])
        xstat = sb("xstat", [P, SLOTS, T, 6])
        xsum, xmean, xdiff = sb("xsum", [P, SLOTS, T]), sb("xmean", [P, SLOTS, T]), sb("xdiff", [P, SLOTS, T])
        xm2, xd2 = sb("xm2", [P, SLOTS, T]), sb("xd2", [P, SLOTS, T])
        xve = sb("xve", [P, SLOTS, T])
        row_gate = sb("row_gate", [P, SLOTS, T])
        xrs = sb("xrs", [P, SLOTS, T])
        st = sb("st", [P, SLOTS, 2, 2, 6])
        mv = sb("mv", [P, SLOTS, 2, 2, 2])
        ve = sb("ve", [P, SLOTS, 2, 2])
        nm = sb("nm", [P, SLOTS, 2, 2])
        nm2 = sb("nm2", [P, SLOTS, 2, 2])
        rs = sb("rs", [P, SLOTS, 2, 2])
        nb = sb("nb", [P, SLOTS, 2, 2])
        x1 = sb("x1", [P, SLOTS, T, D])
        zn = sb("zn", [P, SLOTS, T, D])
        hT = qT
        uT = kT
        q_int = x1[:, :, :, :].rearrange("p s t d -> p (s t) d").bitcast(I32)
        q_int2 = zn[:, :, :, :].rearrange("p s t d -> p (s t) d").bitcast(I32)
        spare = q_wide[:, 1].rearrange("p f h s -> p (f h s)")
        at = [0]

        def take(n):
            at[0] += n
            return spare[:, at[0] - n:at[0]]

        w_scale = take(LAYERS * NF * D).rearrange("p (l k o) -> p l k o", l=LAYERS, k=NF)
        w_unit = take(2 * NF * D).rearrange("p (b k o) -> p b k o", b=2, k=NF)
        la = take(LAYERS * D)[0:RANK].rearrange("p (l o) -> p l o", l=LAYERS)
        lbt = take(LAYERS * D)[0:RANK].rearrange("p (l o) -> p l o", l=LAYERS)
        bias_f = take(BLOCKS * D).rearrange("p (b o) -> p b o", b=BLOCKS)

        bank = [es.enter_context(nc.psum_tensor(f"bank{i}", [P, 512], F32)) for i in range(8)]

        const_in, tab_in, vec_in, gate_in = sem("const_in"), sem("tab_in"), sem("vec_in"), sem("gate_in")
        q_in, scale_in, lora_in, bias_in = sem("q_in"), sem("scale_in"), sem("lora_in"), sem("bias_in")
        x_in, ctx_in, wide_in = per_slot("x_in"), per_slot("ctx_in"), per_slot("wide_in")
        zn_moved = sem("zn_moved")
        v_zero, v_ready, wide_zero, ones_set, half_set = sem("v_zero"), sem("v_ready"), sem("wide_zero"), sem("ones_set"), sem("half_set")
        gate_tanh = sem("gate_tanh")
        bias_split, bias_set = sem("bias_split"), sem("bias_set")
        w_deq, w_scaled, lora_ps, w_ready = sem("w_deq"), sem("w_scaled"), sem("lora_ps"), sem("w_ready")
        x_stat, x_sum, x_mean, x_var = sem("x_stat"), sem("x_sum"), sem("x_mean"), sem("x_var")
        x_ve, x_rs, rg_ready = sem("x_ve"), sem("x_rs"), sem("rg_ready")
        q_mul, q_ready, k_mul, k_ready = sem("q_mul"), sem("q_ready"), sem("k_mul"), sem("k_ready")
        t_ps, t_ev = sem("t_ps"), sem("t_ev")
        score_ps, score_ev = sem("score_ps"), sem("score_ev")
        state_ps, state_ev = sem("state_ps"), sem("state_ev")
        intra_ps, intra_ev = sem("intra_ps"), sem("intra_ev")
        tok_ps, x1_ready = sem("tok_ps"), sem("x1_ready")
        ln_st, ln_mv, ln_ve, ln_rs, ln_nb = sem("ln_st"), sem("ln_mv"), sem("ln_ve"), sem("ln_rs"), sem("ln_nb")
        zn_ready = sem("zn_ready")
        h_ps, h_ev_act, h_ev_dve = sem("h_ps"), sem("h_ev_act"), sem("h_ev_dve")
        y1_ps, z_ps, u_ready, y2_ps, h_res = sem("y1_ps"), sem("z_ps"), sem("u_ready"), sem("y2_ps"), sem("h_res")
        o_ps, o_ev = sem("o_ps"), sem("o_ev")

        x_v = x_d.rearrange("b (t p) d -> b p t d", p=P)
        ctx_v = ctx_d.rearrange("b (t p) d -> b p t d", p=P)
        out_v = out_d.rearrange("b (t p) d -> b p t d", p=P)

        def ln_event(k, s, d):
            return (k * SLOTS + s) * 2 + d

        LN_EVENTS = LN_PASSES * SLOTS * 2

        block = es.enter_context(nc.Block())

        @block.sync
        def _(sp):
            def load_pair(p):
                for s in range(SLOTS):
                    b = SLOTS * p + s
                    sp.dma_start(x[:, s], x_v[b]).then_inc(x_in[s], 16)
                    sp.dma_start(ctx[:, s], ctx_v[b]).then_inc(ctx_in[s], 16)

            def pair(p, more):
                sp.wait_ge(zn_moved, 16 + 16 * SLOTS * p)
                for s in range(SLOTS):
                    sp.wait_ge(t_ev, 2 * UNITS * p + 2 * T * (s + 1))
                    for h in range(HH):
                        rows = slice(h * HD, (h + 1) * HD)
                        sp.dma_start(q_wide[rows, s, :, h, :], qT[rows, s]).then_inc(wide_in[s], 16)
                if more:
                    sp.wait_ge(x1_ready, UNITS * (p + 1))
                    load_pair(p + 1)
                for s in range(SLOTS):
                    sp.wait_ge(o_ev, 2 * SLOTS * p + 2 * (s + 1))
                    sp.dma_start(out_v[SLOTS * p + s], zn[:, s]).then_inc(zn_moved, 16)

            sp.dma_start(q_int, q_d[:, 0:8, :]).then_inc(q_in, 16)
            sp.dma_start(q_int2[:, 0:4, :], q_d[:, 8:12, :]).then_inc(zn_moved, 16)
            for g in range(P // GROUP):
                for k in range(NF):
                    sp.dma_start(w_scale[g * GROUP:(g + 1) * GROUP, :, k, :],
                                 scale_d[:, k * (P // GROUP) + g, :].partition_broadcast(GROUP)).then_inc(scale_in, 16)
            load_pair(0)
            sp.wait_ge(wide_zero, 2)
            with sp.Fori(0, PAIRS - 1) as p:
                pair(p, True)
            pair(PAIRS - 1, False)
            sp.wait_ge(zn_moved, 16 + 16 * SLOTS * PAIRS)

        @block.gpsimd
        def _(pool):
            def prepare_k(p, s, t):
                n = UNITS * p + T * s + t
                pool.wait_ge(ctx_in[s], 16 * p + 16)
                pool.tensor_tensor(k_prod[:, t % 2], ctx[:, s, t, :].unsqueeze(1).broadcast_to([P, 2, D]),
                                   tab[:, t, 2:4, :], ALU.mult).then_inc(k_mul, 1)
                pool.wait_ge(k_mul, n + 1)
                pairs = k_prod[:, t % 2].rearrange("p a (i r) -> p a i r", r=2)
                pool.tensor_tensor(kr[:, s, t, :].rearrange("p (i r) -> p i r", r=2), pairs[:, 0],
                                   pairs[:, 1, :, ::-1], ALU.add).then_inc(k_ready, 1)

            def gate_rows(p, s):
                pool.wait_ge(x_ve, SLOTS * p + s + 1)
                pool.tensor_tensor(xrs[:, s, :], xve[:, s, :], minus_half[:, :], ALU.pow).then_inc(x_rs, 1)
                pool.wait_ge(x_rs, SLOTS * p + s + 1)
                pool.tensor_tensor(row_gate[:, s, :], xrs[:, s, :], tanh_gate[:, 0:1].broadcast_to([P, T]),
                                   ALU.mult).then_inc(rg_ready, 1)

            def inverse_std(p, e):
                s, d = e // 2 % SLOTS, e % 2
                n = LN_EVENTS * p + e
                pool.wait_ge(ln_ve, 2 * n + 2)
                pool.tensor_tensor(rs[:, s, d], ve[:, s, d], minus_half[:, 0:2], ALU.pow).then_inc(ln_rs, 1)
                pool.wait_ge(ln_rs, n + 1)
                pool.tensor_tensor(nb[:, s, d], nm[:, s, d], rs[:, s, d], ALU.mult).then_inc(ln_nb, 1)

            def pair(p, more):
                for e in range(2 * SLOTS):
                    inverse_std(p, e)
                todo = [(s, t) for s in range(SLOTS) for t in range(T)]
                for blk in range(BLOCKS):
                    for s in range(SLOTS):
                        for d in range(2):
                            inverse_std(p, ln_event(blk + 1, s, d))
                        for s2, t2 in todo[:2] if more else []:
                            prepare_k(p + 1, s2, t2)
                        todo = todo[2:]
                for s in range(SLOTS) if more else []:
                    gate_rows(p + 1, s)

            pool.memset(minus_half[:, :], -0.5).then_inc(half_set, 1)
            pool.memset(ones[:, :], 1.0).then_inc(ones_set, 1)
            pool.memset(q_wide[:, 0].rearrange("p f h s -> p (f h s)"), 0.0).then_inc(wide_zero, 1)
            pool.wait_ge(w_ready, LAYERS)
            pool.wait_ge(bias_split, 6)
            pool.memset(q_wide[:, 1].rearrange("p f h s -> p (f h s)"), 0.0).then_inc(wide_zero, 1)
            pool.wait_ge(half_set, 1)
            pool.wait_ge(tab_in, 16)
            pool.wait_ge(gate_tanh, 1)
            for s in range(SLOTS):
                for t in range(T):
                    prepare_k(0, s, t)
                gate_rows(0, s)
            with pool.Fori(0, PAIRS - 1) as p:
                pair(p, True)
            pair(PAIRS - 1, False)

        @block.scalar
        def _(act):
            act.dma_start(const[:, :], const_d).then_inc(const_in, 16)
            act.dma_start(la[:, :, :], la_d).then_inc(lora_in, 16)
            act.dma_start(lbt[:, :, :], lbt_d).then_inc(lora_in, 16)
            act.dma_start(tab[:, :, :, :], tab_d).then_inc(tab_in, 16)
            act.dma_start(gate[:, :], gates_d.partition_broadcast(P)).then_inc(gate_in, 16)
            act.dma_start(vec[:, :, :, :], vec_d).then_inc(vec_in, 16)
            act.dma_start(bias_f[:, :, :], bias_d.partition_broadcast(P)).then_inc(bias_in, 16)
            act.wait_ge(gate_in, 16)
            act.activation(tanh_gate[:, :], gate[:, :], ACT.Tanh).then_inc(gate_tanh, 1)
            act.wait_ge(vec_in, 16)

            def normalise(p, e, src):
                s, d = e // 2 % SLOTS, e % 2
                act.wait_ge(ln_nb, LN_EVENTS * p + e + 1)
                for i in range(2):
                    act.activation(zn[:, s, 2 * d + i, :], src(s, d, i), ACT.Identity,
                                   bias=nb[:, s, d, i:i + 1], scale=rs[:, s, d, i:i + 1]).then_inc(zn_ready, 1)

            def from_x1(s, d, i):
                return x1[:, s, 2 * d + i, :]

            def from_y1(s, d, i):
                return bank[2 * s + d][:, i * D:(i + 1) * D]

            def evacuate_intra(p, u):
                act.wait_ge(intra_ps, 2 * UNITS * p + 2 * u + 2)
                if u >= 2:
                    act.wait_ge(tok_ps, UNITS * p + u - 1)
                act.activation(intra[:, u % 2].rearrange("p g n -> p (g n)"), bank[2 + u % 2][:, 0:256],
                               ACT.Copy).then_inc(intra_ev, 1)

            def spread_values(p, s):
                act.wait_ge(ctx_in[s], 16 * p + 16)
                for c in range(NC):
                    rows = slice(c * C, (c + 1) * C)
                    act.activation(v_chunk[rows, s, :, :, c, :].rearrange("p t h e -> p (t h) e"),
                                   ctx[rows, s].rearrange("p t (h e) -> p (t h) e", e=HD),
                                   ACT.Copy).then_inc(v_ready, 1)

            def gelu(p, blk, s):
                n = (BLOCKS * p + blk) * SLOTS + s
                act.wait_ge(z_ps, n + 1)
                for f in range(NF):
                    act.activation(uT[:, s, f, :], bank[4 + 2 * s + f][:, :], ACT.Gelu,
                                   bias=vec[:, 1, blk, f:f + 1], scale=vec[:, 0, blk, f:f + 1]).then_inc(u_ready, 1)

            def pair(p, more):
                for u in range(UNITS):
                    s, t = u // T, u % T
                    act.wait_ge(t_ps, UNITS * p + u + 1)
                    src = bank[4 + t][:, :].rearrange("p (a n) -> p a n", a=4)
                    cols = slice(t * P, (t + 1) * P)
                    act.activation(qT[:, s, :, cols], src[:, 0:NF], ACT.Copy).then_inc(t_ev, 1)
                    act.activation(kT[:, s, :, cols], src[:, NF:2 * NF], ACT.Copy).then_inc(t_ev, 1)
                for u in range(UNITS):
                    evacuate_intra(p, u)
                    if u == T + 1:
                        for d in range(2):
                            normalise(p, ln_event(0, 0, d), from_x1)
                for d in range(2):
                    normalise(p, ln_event(0, 1, d), from_x1)
                for s in range(SLOTS):
                    act.wait_ge(h_ps, SLOTS * p + s + 1)
                    act.activation(hT[:, s, 0, :], bank[4 + 2 * s][:, :], ACT.Copy).then_inc(h_ev_act, 1)
                    if s == 0:
                        for d in range(2):
                            normalise(p, ln_event(1, 0, d), from_y1)
                for blk in range(BLOCKS):
                    gelu(p, blk, 0)
                    if more and blk >= 1:
                        spread_values(p + 1, blk - 1)
                    for d in range(2):
                        normalise(p, ln_event(blk + 1, 1, d), from_y1)
                    gelu(p, blk, 1)
                    if blk + 1 < BLOCKS:
                        for d in range(2):
                            normalise(p, ln_event(blk + 2, 0, d), from_y1)

            act.wait_ge(v_zero, 1)
            for s in range(SLOTS):
                spread_values(0, s)
            with act.Fori(0, PAIRS - 1) as p:
                pair(p, True)
            pair(PAIRS - 1, False)

        @block.vector
        def _(dve):
            def prepare_q(p, s, t):
                n = UNITS * p + T * s + t
                dve.wait_ge(x_in[s], 16 * p + 16)
                dve.bn_stats(xstat[:, s, t, :], x[:, s, t, :]).then_inc(x_stat, 1)
                dve.wait_ge(x_stat, n + 1)
                dve.tensor_tensor(xsum[:, s, t:t + 1], xstat[:, s, t, 1:2], xstat[:, s, t, 4:5],
                                  ALU.add).then_inc(x_sum, 1)
                dve.wait_ge(x_sum, n + 1)
                dve.tensor_scalar(xmean[:, s, t:t + 1], xsum[:, s, t:t + 1], 0.5, None, ALU.mult).then_inc(x_mean, 1)
                dve.wait_ge(x_mean, n + 1)
                dve.scalar_tensor_tensor(q_prod[:, t % 2], x[:, s, t, :].unsqueeze(1).broadcast_to([P, 2, D]),
                                         xmean[:, s, t:t + 1], tab[:, t, 0:2, :], ALU.subtract,
                                         ALU.mult).then_inc(q_mul, 1)
                dve.wait_ge(q_mul, n + 1)
                pairs = q_prod[:, t % 2].rearrange("p a (i r) -> p a i r", r=2)
                dve.tensor_tensor(qr[:, s, t, :].rearrange("p (i r) -> p i r", r=2), pairs[:, 0],
                                  pairs[:, 1, :, ::-1], ALU.add).then_inc(q_ready, 1)
                if t == T - 1:
                    m = SLOTS * p + s
                    dve.tensor_tensor(xdiff[:, s, :], xstat[:, s, :, 1], xstat[:, s, :, 4],
                                      ALU.subtract).then_inc(x_var, 1)
                    dve.scalar_tensor_tensor(xm2[:, s, :], xstat[:, s, :, 2], D * LN_EPS, xstat[:, s, :, 5],
                                             ALU.add, ALU.add).then_inc(x_var, 1)
                    dve.wait_ge(x_var, 3 * m + 2)
                    dve.scalar_tensor_tensor(xd2[:, s, :], xdiff[:, s, :], 0.25, xdiff[:, s, :],
                                             ALU.mult, ALU.mult).then_inc(x_var, 1)
                    dve.wait_ge(x_var, 3 * m + 3)
                    dve.scalar_tensor_tensor(xve[:, s, :], xm2[:, s, :], 1.0 / D, xd2[:, s, :],
                                             ALU.mult, ALU.add).then_inc(x_ve, 1)

            def statistics(p, e, src):
                s, d = e // 2 % SLOTS, e % 2
                m = LN_EVENTS * p + e
                n = 2 * m
                for i in range(2):
                    dve.bn_stats(st[:, s, d, i, :], src(s, d, i)).then_inc(ln_st, 1)
                dve.wait_ge(ln_st, n + 2)
                dve.scalar_tensor_tensor(nm2[:, s, d], st[:, s, d, :, 1], -1.0, st[:, s, d, :, 4],
                                         ALU.mult, ALU.subtract).then_inc(ln_mv, 1)
                for i in range(2):
                    dve.bn_aggr(mv[:, s, d, i, :], st[:, s, d, i, :]).then_inc(ln_mv, 1)
                dve.wait_ge(ln_mv, 3 * m + 3)
                dve.tensor_scalar(ve[:, s, d], mv[:, s, d, :, 1], LN_EPS, None, ALU.add).then_inc(ln_ve, 1)
                dve.tensor_scalar(nm[:, s, d], nm2[:, s, d], 0.5, None, ALU.mult).then_inc(ln_ve, 1)

            def x1_statistics(p, s):
                for d in range(2):
                    dve.wait_ge(x1_ready, UNITS * p + T * s + 2 * d + 2)
                    statistics(p, ln_event(0, s, d), lambda s, d, i: x1[:, s, 2 * d + i, :])

            def y1_statistics(p, blk, s):
                for d in range(2):
                    dve.wait_ge(y1_ps, ((BLOCKS * p + blk) * SLOTS + s) * 2 + d + 1)
                    statistics(p, ln_event(blk + 1, s, d), lambda s, d, i: bank[2 * s + d][:, i * D:(i + 1) * D])

            def evacuate_scores(p, i):
                dve.wait_ge(score_ps, 2 * UNITS * p + i + 1)
                if i >= 2:
                    dve.wait_ge(intra_ps, 2 * UNITS * p + i - 1)
                dve.tensor_tensor(sT[:, i % 2], bank[i % 2][:, :].rearrange("p (h n) -> p h n", h=HH),
                                  causal.unsqueeze(1).broadcast_to([P, HH, C]), ALU.mult).then_inc(score_ev, 1)

            def evacuate_state(p, s, k):
                n = (NC * T - 1) * (SLOTS * p + s) + k
                dve.wait_ge(state_ps, n + 1)
                u_read = T * s + (k - 3) // NC
                if k >= 3:
                    dve.wait_ge(tok_ps, UNITS * p + u_read + 1)
                dve.tensor_tensor(state[:, s, (k + 1) % 4], bank[6 + s][:, 0:256].rearrange("p (f n) -> p f n", f=NF),
                                  diag16.unsqueeze(1).broadcast_to([P, NF, P]), ALU.mult).then_inc(state_ev, 1)

            def residual_x1(p, u):
                s, t = u // T, u % T
                dve.wait_ge(tok_ps, UNITS * p + u + 1)
                dve.scalar_tensor_tensor(x1[:, s, t, :], bank[4 + u % 2][:, 0:256], row_gate[:, s, t:t + 1],
                                         x[:, s, t, :], ALU.mult, ALU.add).then_inc(x1_ready, 1)

            def evacuate_h(p, s):
                dve.wait_ge(h_ps, SLOTS * p + s + 1)
                dve.tensor_copy(hT[:, s, 1, :], bank[5 + 2 * s][:, :]).then_inc(h_ev_dve, 1)

            def residual_h(p, blk, s):
                n = (BLOCKS * p + blk) * SLOTS + s
                for f in range(NF):
                    dve.wait_ge(y2_ps, NF * n + f + 1)
                    dve.scalar_tensor_tensor(hT[:, s, f, :], bank[2 * s + f][:, :], vec[:, 2, blk, f:f + 1],
                                             hT[:, s, f, :], ALU.add, ALU.add).then_inc(h_res, 1)

            def output(p, s):
                for d in range(2):
                    dve.wait_ge(o_ps, (SLOTS * p + s) * 2 + d + 1)
                    dve.scalar_tensor_tensor(zn[:, s, 2 * d:2 * d + 2, :].rearrange("p t d -> p (t d)"),
                                             bank[4 + 2 * s + d][:, :], tanh_gate[:, 1:2],
                                             x1[:, s, 2 * d:2 * d + 2, :].rearrange("p t d -> p (t d)"),
                                             ALU.mult, ALU.add).then_inc(o_ev, 1)

            def pair(p, more):
                dve.wait_ge(rg_ready, SLOTS * (p + 1))
                for i in range(2 * UNITS):
                    u, f = i // 2, i % 2
                    s, t = u // T, u % T
                    evacuate_scores(p, i)
                    k = NC * t + f
                    if k < NC * T - 1:
                        evacuate_state(p, s, k)
                    if f == 1 and u >= 1:
                        residual_x1(p, u - 1)
                        if u == T:
                            x1_statistics(p, 0)
                residual_x1(p, UNITS - 1)
                x1_statistics(p, 1)

                todo = [(s, t) for s in range(SLOTS) for t in range(T)] if more else []

                def prepare_next():
                    if todo:
                        prepare_q(p + 1, *todo.pop(0))

                evacuate_h(p, 0)
                y1_statistics(p, 0, 0)
                evacuate_h(p, 1)
                for blk in range(BLOCKS):
                    prepare_next()
                    y1_statistics(p, blk, 1)
                    residual_h(p, blk, 0)
                    prepare_next()
                    if blk + 1 < BLOCKS:
                        y1_statistics(p, blk + 1, 0)
                    else:
                        output(p, 0)
                    prepare_next()
                    residual_h(p, blk, 1)
                output(p, 1)

            dve.memset(v_chunk[:, :, :, :, :, :].rearrange("p s t h c e -> p (s t h c e)"), 0.0).then_inc(v_zero, 1)
            dve.memset(bias_rows[:, :, :].rearrange("p b d -> p (b d)"), 0.0).then_inc(bias_set, 1)
            dve.wait_ge(bias_in, 16)
            dve.wait_ge(bias_set, 1)
            for j in range(3):
                dve.tensor_copy(bias_h[:, :, :], bias_f[:, :, :]).then_inc(bias_split, 1)
                dve.wait_ge(bias_split, 2 * j + 1)
                dve.tensor_copy(bias_rows[32 * j:32 * j + 1], bias_h[32 * j:32 * j + 1]).then_inc(bias_set, 1)
                dve.tensor_tensor(bias_f[:, :, :], bias_f[:, :, :], bias_h[:, :, :],
                                  ALU.subtract).then_inc(bias_split, 1)
                dve.wait_ge(bias_split, 2 * j + 2)
                dve.wait_ge(bias_set, j + 2)
            dve.wait_ge(q_in, 16)
            dve.wait_ge(zn_moved, 16)
            dve.wait_ge(scale_in, 16 * P // GROUP * NF)
            for l in range(LAYERS):
                src = q_int[:, 2 * l:2 * l + 2, :] if l < 4 else q_int2[:, 2 * l - 8:2 * l - 6, :]
                if l >= 2:
                    dve.wait_ge(w_scaled, l - 1)
                dve.tensor_scalar(w_unit[:, l % 2], src, 1.0 / 7.5, -1.0, ALU.mult, ALU.add).then_inc(w_deq, 1)
                dve.wait_ge(w_deq, l + 1)
                dve.tensor_tensor(wt[:, l], w_unit[:, l % 2], w_scale[:, l], ALU.mult).then_inc(w_scaled, 1)
                dve.wait_ge(w_scaled, l + 1)
                dve.wait_ge(lora_ps, l + 1)
                dve.tensor_tensor(wt[:, l].rearrange("p k o -> p (k o)"), bank[l % 4][:, :],
                                  wt[:, l].rearrange("p k o -> p (k o)"), ALU.add).then_inc(w_ready, 1)
            dve.wait_ge(tab_in, 16)
            for s in range(SLOTS):
                for t in range(T):
                    prepare_q(0, s, t)
            dve.wait_ge(gate_tanh, 1)
            dve.wait_ge(const_in, 16)
            dve.wait_ge(vec_in, 16)
            with dve.Fori(0, PAIRS - 1) as p:
                pair(p, True)
            pair(PAIRS - 1, False)

        @block.tensor
        def _(pe):
            def transpose_qk(p, u):
                s, t = u // T, u % T
                n = UNITS * p + u
                pe.wait_ge(q_ready, n + 1)
                pe.wait_ge(k_ready, n + 1)
                if s >= 1:
                    pe.wait_ge(t_ev, 2 * (n - T) + 2)
                for a, src in enumerate((qr, kr)):
                    for f in range(NF):
                        col = (a * NF + f) * P
                        last = pe.transpose(bank[4 + t][:, col:col + P], src[:, s, t, f * P:(f + 1) * P], ident)
                last.then_inc(t_ps, 1)

            def scores(p, i):
                u, f = i // 2, i % 2
                s, t = u // T, u % T
                if u % T == 0 and f == 0:
                    pe.wait_ge(wide_in[s], 16 * HH * (p + 1))
                    pe.wait_ge(t_ev, 2 * UNITS * p + 2 * T * (s + 1))
                    pe.wait_ge(v_ready, NC * (SLOTS * p + s + 1))
                    pe.wait_ge(ctx_in[s], 16 * (p + 1))
                if i >= 2:
                    pe.wait_ge(score_ev, 2 * UNITS * p + i - 1)
                for c in range(NC):
                    cols = slice(t * P + c * C, t * P + (c + 1) * C)
                    last = pe.matmul(bank[i % 2][c * C:(c + 1) * C, :], kT[:, s, f, cols], q_wide[:, s, f, :, cols],
                                     start=True, stop=True)
                last.then_inc(score_ps, 1)

            def update_state(p, s, k):
                t, c = k // NC, k % NC
                n = (NC * T - 1) * (SLOTS * p + s) + k
                if k >= 1:
                    pe.wait_ge(state_ev, n)
                elif s == 0:
                    pe.wait_ge(t_ev, 2 * UNITS * (p + 1))
                rows = slice(c * C, (c + 1) * C)
                for f in range(NF):
                    feats = slice(f * P, (f + 1) * P)
                    last = pe.matmul(bank[6 + s][:, feats], kr[rows, s, t, feats], ctx[rows, s, t, feats],
                                     start=(k == 0 and f == 0), stop=(k == NC * T - 2), skip_group_check=True)
                last.then_inc(state_ps, 1)

            def intra_chunk(p, i):
                u, f = i // 2, i % 2
                s, t = u // T, u % T
                pe.wait_ge(score_ev, 2 * UNITS * p + i + 1)
                if f == 0 and u >= 2:
                    pe.wait_ge(intra_ev, UNITS * p + u - 1)
                for h in range(HH):
                    head = HH * f + h
                    j, g = head % 4, head // 4
                    last = pe.matmul(bank[2 + u % 2][32 * j:32 * (j + 1), g * C:(g + 1) * C],
                                     v_chunk[:, s, t, head].rearrange("p c e -> p (c e)"), sT[:, i % 2, h, :],
                                     start=True, stop=True)
                last.then_inc(intra_ps, 1)

            def to_tokens(p, u):
                s, t = u // T, u % T
                pe.wait_ge(intra_ev, UNITS * p + u + 1)
                if u >= 2:
                    pe.wait_ge(x1_ready, UNITS * p + u - 1)
                k = min(NC * t, NC * T - 2)
                pe.wait_ge(state_ev, (NC * T - 1) * (SLOTS * p + s) + k + 1)
                out = bank[4 + u % 2]
                for c in range(NC):
                    chunk = NC * t + c
                    rows = slice(c * C, (c + 1) * C)
                    first = True
                    if chunk > 0:
                        for f in range(NF):
                            pe.matmul(out[rows, f * P:(f + 1) * P], qT[:, s, f, chunk * C:(chunk + 1) * C],
                                      state[:, s, chunk % 4, f, :], start=first, stop=False, skip_group_check=True)
                            first = False
                    for g in range(HEADS // 4):
                        last = pe.matmul(out[rows, g * C:(g + 1) * C], intra[:, u % 2, g, :], pick[:, c, :],
                                         start=first, stop=True, skip_group_check=True)
                        first = False
                last.then_inc(tok_ps, 1)

            def transpose_tiles(src, s, done):
                for t in range(T):
                    for f in range(NF):
                        last = pe.transpose(bank[4 + 2 * s + f][:, t * P:(t + 1) * P],
                                            src[:, s, t, f * P:(f + 1) * P], ident)
                last.then_inc(done, 1)

            def h_to_features(p, s):
                pe.wait_ge(zn_ready, 2 * LN_EVENTS * p + 2 * ln_event(0, s, 1) + 2)
                pe.wait_ge(x1_ready, UNITS * (p + 1))
                transpose_tiles(zn, s, h_ps)

            def linear1(p, blk, s):
                n = (BLOCKS * p + blk) * SLOTS + s
                if blk == 0:
                    pe.wait_ge(h_ev_act, SLOTS * p + s + 1)
                    pe.wait_ge(h_ev_dve, SLOTS * p + s + 1)
                else:
                    pe.wait_ge(h_res, NF * (n - SLOTS) + NF)
                for t in range(T):
                    out = bank[2 * s + t // 2][:, (t % 2) * D:(t % 2 + 1) * D]
                    for f in range(NF):
                        pe.matmul(out, hT[:, s, f, t * P:(t + 1) * P], wt[:, 2 * blk, f, :], start=(f == 0), stop=False)
                    last = pe.matmul(out, ones[:, :], bias_rows[:, blk, :], start=False, stop=True)
                    if t % 2 == 1:
                        last.then_inc(y1_ps, 1)

            def z_to_features(p, blk, s):
                pe.wait_ge(zn_ready, 2 * LN_EVENTS * p + 2 * ln_event(blk + 1, s, 1) + 2)
                transpose_tiles(zn, s, z_ps)

            def linear2(p, blk, s):
                n = (BLOCKS * p + blk) * SLOTS + s
                pe.wait_ge(u_ready, NF * n + NF)
                for f in range(NF):
                    for k in range(NF):
                        last = pe.matmul(bank[2 * s + f][:, :], wt[:, 2 * blk + 1, k, f * P:(f + 1) * P],
                                         uT[:, s, k, :], start=(k == 0), stop=(k == NF - 1))
                    last.then_inc(y2_ps, 1)

            def h_to_tokens(p, s):
                n = (BLOCKS * p + BLOCKS - 1) * SLOTS + s
                pe.wait_ge(h_res, NF * n + NF)
                for t in range(T):
                    for f in range(NF):
                        col = (t % 2) * D + f * P
                        last = pe.transpose(bank[4 + 2 * s + t // 2][:, col:col + P],
                                            hT[:, s, f, t * P:(t + 1) * P], ident)
                    if t % 2 == 1:
                        last.then_inc(o_ps, 1)

            def pair(p):
                for u in range(UNITS):
                    transpose_qk(p, u)
                for i in range(2 * UNITS):
                    u, f = i // 2, i % 2
                    s, t = u // T, u % T
                    scores(p, i)
                    k = NC * t + f
                    if k < NC * T - 1:
                        update_state(p, s, k)
                    if i >= 1:
                        intra_chunk(p, i - 1)
                    if f == 1 and u >= 1:
                        to_tokens(p, u - 1)
                intra_chunk(p, 2 * UNITS - 1)
                to_tokens(p, UNITS - 1)

                h_to_features(p, 0)
                linear1(p, 0, 0)
                h_to_features(p, 1)
                for blk in range(BLOCKS):
                    z_to_features(p, blk, 0)
                    linear1(p, blk, 1)
                    linear2(p, blk, 0)
                    z_to_features(p, blk, 1)
                    if blk + 1 < BLOCKS:
                        linear1(p, blk + 1, 0)
                    else:
                        h_to_tokens(p, 0)
                    linear2(p, blk, 1)
                h_to_tokens(p, 1)
                pe.wait_ge(o_ev, 2 * SLOTS * (p + 1))

            pe.wait_ge(lora_in, 32)
            for l in range(LAYERS):
                if l >= 4:
                    pe.wait_ge(w_ready, l - 3)
                for k in range(NF):
                    last = pe.matmul(bank[l % 4][:, k * D:(k + 1) * D], la[:, l, k * P:(k + 1) * P], lbt[:, l, :],
                                     start=True, stop=True)
                last.then_inc(lora_ps, 1)
            pe.wait_ge(const_in, 16)
            pe.wait_ge(w_ready, LAYERS)
            pe.wait_ge(bias_set, 4)
            pe.wait_ge(ones_set, 1)
            with pe.Fori(0, PAIRS - 1) as p:
                pair(p)
            pair(PAIRS - 1)


def constants():
    f = np.float32
    lin = np.linspace(np.log(1.0 / 32.0), np.log(1.0 / 512.0), HEADS).astype(f)
    gamma = (f(1.0) - np.exp(lin)).astype(f).astype(np.float64)
    pos = np.arange(S, dtype=f)
    base = ((np.arange(0, HD, 2, dtype=f) + f(0.4 * HD)) / f(1.4 * HD)).astype(np.float64)
    scale = base[None, :] ** (pos.astype(np.float64) / 512.0)[:, None]
    inv_freq = (1.0 / 10000.0 ** (np.arange(HD // 2, dtype=f) / f(HD // 2))).astype(f)
    angle = (pos[:, None] * inv_freq[None, :]).astype(f).astype(np.float64)
    decay = gamma[None, :] ** (pos.astype(np.float64) - S // 2)[:, None]

    def table(trig, sign, scl, dec):
        return dec[:, :, None, None] * (trig * scl)[:, None, :, None] * np.array(sign)[None, None, None, :]

    tabs = [table(np.cos(angle), [1, 1], scale, decay), table(np.sin(angle), [1, -1], scale, decay),
            table(np.cos(angle), [1, 1], 1 / scale, 1 / decay), table(np.sin(angle), [1, -1], 1 / scale, 1 / decay)]
    tab = np.stack([a.reshape(T, P, D) for a in tabs], axis=2).transpose(1, 0, 2, 3)
    i = np.arange(P)
    const = np.zeros((P, C_END), f)
    const[:, C_ID:C_ID + P] = np.eye(P)
    const[:, C_DIAG:C_DIAG + P] = i[:, None] // HD == i[None, :] // HD
    for c in range(NC):
        for j in range(4):
            for e in range(HD):
                const[32 * j + HD * c + e, C_PICK + c * C + HD * j + e] = 1
    const[:, C_CAUSAL:C_CAUSAL + C] = np.arange(C)[None, :] >= i[:, None] % C
    return const, np.ascontiguousarray(tab.astype(f))


def kernel(x, ctx_1024, g_xattn, g_ffn, L0_ffn_qweights, L0_ffn_scales, L0_ffn_biases, L0_ffn_lora_a, L0_ffn_lora_b,
           L0_ffn_ln_gamma, L0_ffn_ln_beta):
    import concourse.bacc as bacc
    from concourse.bass_utils import run_bass_kernel_spmd

    def c(a):
        return np.ascontiguousarray(a)

    const, tab = constants()
    q, biases = np.asarray(L0_ffn_qweights), np.asarray(L0_ffn_biases)
    vec = np.stack([np.asarray(L0_ffn_ln_gamma), np.asarray(L0_ffn_ln_beta), biases[1::2]])
    arrays = {
        "x": c(x), "ctx": c(ctx_1024),
        "gates": c(np.concatenate([np.asarray(g_xattn), np.asarray(g_ffn)])),
        "qweights": c(q.transpose(2, 0, 1).reshape(NF, P, LAYERS, D).transpose(1, 2, 0, 3).reshape(P, LAYERS * NF, D)),
        "scales": c(np.asarray(L0_ffn_scales).transpose(0, 2, 1)),
        "bias1": c(biases[0::2]),
        "lora_a": c(np.asarray(L0_ffn_lora_a).transpose(1, 0, 2)),
        "lora_bt": c(np.asarray(L0_ffn_lora_b).transpose(2, 0, 1)),
        "vectors": c(vec.reshape(3, BLOCKS, NF, P).transpose(3, 0, 1, 2)),
        "const": const, "tables": tab,
    }
    nc = bacc.Bacc("TRN2", target_bir_lowering=False, num_devices=1)
    args = [nc.dram_tensor(f"in_{k}", a.shape, mybir.dt.from_np(a.dtype), kind="ExternalInput").ap()
            for k, a in arrays.items()]
    out = nc.dram_tensor("out", (B, S, D), F32, kind="ExternalOutput").ap()
    build(nc, *args, out)
    r = run_bass_kernel_spmd(nc, [{f"in_{k}": a for k, a in arrays.items()}], core_ids=[0])
    return r.results[0]["out"]
```

```python
from contextlib import ExitStack

import numpy as np

import concourse.bass as bass
from concourse import mybir
from concourse.alu_op_type import AluOpType as ALU

F32 = mybir.dt.float32
BF16 = mybir.dt.bfloat16
I32 = mybir.dt.int32
ACT = mybir.ActivationFunctionType

B, S, D = 8, 512, 256
HEADS, HD = 16, 16
P = 128
T = S // P
NF = D // P
C = 64
NC = P // C
HH = HEADS // NF
SLOTS = 2
PAIRS = B // SLOTS
UNITS = SLOTS * T
PAIR_W = 2 * HD
BLOCKS = 3
LORA_ROWS = 3
LAYERS = 2 * BLOCKS
RANK = 32
GROUP = 16
BIAS_ROWS = 65
LN_EPS = 1e-5
LN_PASSES = BLOCKS + 1

C_ID, C_DIAG, C_PICK, C_CAUSAL, C_END = 0, P, 2 * P, 3 * P, 3 * P + C


def build(nc, x_d, ctx_d, gates_d, q_d, scale_d, bias_d, la_d, lbt_d, vec_d, const_d, tab_d, out_d):
    es = ExitStack()
    with es:
        def sb(name, shape, dt=F32):
            return es.enter_context(nc.sbuf_tensor(name, shape, dt))

        def sem(name):
            return es.enter_context(nc.semaphore(name))

        def per_slot(name):
            return [sem(f"{name}{s}") for s in range(SLOTS)]

        const = sb("const", [P, C_END])
        ident = const[:, C_ID:C_ID + P]
        diag16 = const[:, C_DIAG:C_DIAG + P]
        pick = const[:, C_PICK:C_PICK + P].rearrange("p (c n) -> p c n", c=NC)
        causal = const[:, C_CAUSAL:C_CAUSAL + C]
        tab = sb("tab", [P, T, 4, D])
        vec = sb("vec", [P, 3, BLOCKS, NF])
        gate = sb("gate", [P, 2])
        tanh_gate = sb("tanh_gate", [P, 2])
        minus_half = sb("minus_half", [P, T])
        wt = sb("wt", [P, LAYERS, NF, D])
        ones = sb("ones", [P, P], BF16)
        bias_h = sb("bias_h", [BIAS_ROWS, BLOCKS, D], BF16)
        bias_rows = sb("bias_rows", [P, BLOCKS, D], BF16)
        x = sb("x", [P, SLOTS, T, D])
        ctx = sb("ctx", [P, SLOTS, T, D])
        v_chunk = sb("v_chunk", [P, SLOTS, T, HEADS, NC, HD])
        qr = sb("qr", [P, SLOTS, T, D])
        kr = sb("kr", [P, SLOTS, T, D])
        q_prod = sb("q_prod", [P, 2, 2, D])
        k_prod = sb("k_prod", [P, 2, 2, D])
        qT = sb("qT", [P, SLOTS, NF, S])
        kT = sb("kT", [P, SLOTS, NF, S])
        q_wide = sb("q_wide", [P, SLOTS, NF, HH, S])
        intra = sb("intra", [P, 2, HEADS // 4, C])
        shared = sb("shared", [P, 4 * NF * S])
        state = shared[:, 0:2 * NF * S].rearrange("p (s r f n) -> p s r f n", s=SLOTS, r=4, f=NF)
        uT = shared[:, 0:2 * NF * S].rearrange("p (s f n) -> p s f n", s=SLOTS, f=NF)
        sT = shared[:, 2 * NF * S:3 * NF * S].rearrange("p (b h n) -> p b h n", b=2, h=HH)
        hT = [shared[:, (3 - s) * NF * S:(4 - s) * NF * S].rearrange("p (f n) -> p f n", f=NF) for s in range(SLOTS)]
        xstat = sb("xstat", [P, SLOTS, T, 6])
        xsum, xmean, xdiff = sb("xsum", [P, SLOTS, T]), sb("xmean", [P, SLOTS, T]), sb("xdiff", [P, SLOTS, T])
        xm2, xd2 = sb("xm2", [P, SLOTS, T]), sb("xd2", [P, SLOTS, T])
        xve = sb("xve", [P, SLOTS, T])
        row_gate = sb("row_gate", [P, SLOTS, T])
        xrs = sb("xrs", [P, SLOTS, T])
        st = sb("st", [P, SLOTS, 2, 2, 6])
        mv = sb("mv", [P, SLOTS, 2, 2, 2])
        ve = sb("ve", [P, SLOTS, 2, 2])
        nm = sb("nm", [P, SLOTS, 2, 2])
        nm2 = sb("nm2", [P, SLOTS, 2, 2])
        rs = sb("rs", [P, SLOTS, 2, 2])
        nb = sb("nb", [P, SLOTS, 2, 2])
        x1 = sb("x1", [P, SLOTS, T, D])
        zn = sb("zn", [P, SLOTS, T, D])
        q_int = x1[:, :, :, :].rearrange("p s t d -> p (s t) d").bitcast(I32)
        q_int2 = zn[:, 0, :, :].bitcast(I32)
        bias_f = zn[0:BIAS_ROWS, 1, 0:BLOCKS, :]
        w_scale = shared[:, 0:NF * LAYERS * D].rearrange("p (k o) -> p k o", k=NF)
        la = shared[:, LAYERS * NF * D:(LAYERS * NF + 2) * D].rearrange("p (j o) -> p j o", j=2)
        lbt = shared[:, (LAYERS * NF + 2) * D:(LAYERS * NF + 4) * D].rearrange("p (j o) -> p j o", j=2)

        bank = [es.enter_context(nc.psum_tensor(f"bank{i}", [P, 512], F32)) for i in range(8)]

        const_in, vec_in, gate_in = sem("const_in"), sem("vec_in"), sem("gate_in")
        tab_in = [sem(f"tab_in{i}") for i in range(T // 2)]
        q_in, scale_in, lora_in, bias_in = sem("q_in"), sem("scale_in"), sem("lora_in"), sem("bias_in")
        x_in, ctx_in, wide_in = per_slot("x_in"), per_slot("ctx_in"), per_slot("wide_in")
        zn_moved = sem("zn_moved")
        v_zero, v_ready, wide_zero, ones_set, half_set = sem("v_zero"), sem("v_ready"), sem("wide_zero"), sem("ones_set"), sem("half_set")
        gate_tanh = sem("gate_tanh")
        bias_split, bias_set = sem("bias_split"), sem("bias_set")
        w_deq, w_scaled, lora_ps, w_ready = sem("w_deq"), sem("w_scaled"), sem("lora_ps"), sem("w_ready")
        x_stat, x_sum, x_mean, x_var = sem("x_stat"), sem("x_sum"), sem("x_mean"), sem("x_var")
        x_ve, x_rs, rg_ready = sem("x_ve"), sem("x_rs"), sem("rg_ready")
        q_mul, q_ready, k_mul, k_ready = sem("q_mul"), sem("q_ready"), sem("k_mul"), sem("k_ready")
        t_ps, t_ev = sem("t_ps"), sem("t_ev")
        score_ps, score_ev = sem("score_ps"), sem("score_ev")
        state_ps, state_ev = sem("state_ps"), sem("state_ev")
        intra_ps, intra_ev = sem("intra_ps"), sem("intra_ev")
        tok_ps, x1_ready = sem("tok_ps"), sem("x1_ready")
        ln_st, ln_mv, ln_ve, ln_rs, ln_nb = sem("ln_st"), sem("ln_mv"), sem("ln_ve"), sem("ln_rs"), sem("ln_nb")
        zn_ready = sem("zn_ready")
        h_ps, h_ev_act, h_ev_dve = sem("h_ps"), sem("h_ev_act"), sem("h_ev_dve")
        y1_ps, z_ps, u_ready, y2_ps, h_res = sem("y1_ps"), sem("z_ps"), sem("u_ready"), sem("y2_ps"), sem("h_res")
        o_ps, o_ev = sem("o_ps"), sem("o_ev")

        x_v = x_d.rearrange("b (t p) d -> b p t d", p=P)
        ctx_v = ctx_d.rearrange("b (t p) d -> b p t d", p=P)
        out_v = out_d.rearrange("b (t p) d -> b p t d", p=P)

        def ln_event(k, s, d):
            return (k * SLOTS + s) * 2 + d

        LN_EVENTS = LN_PASSES * SLOTS * 2

        block = es.enter_context(nc.Block())

        @block.sync
        def _(sp):
            def load_x(p, s):
                sp.dma_start(x[:, s], x_v[SLOTS * p + s]).then_inc(x_in[s], 16)

            def load_ctx(p, s):
                sp.dma_start(ctx[:, s], ctx_v[SLOTS * p + s]).then_inc(ctx_in[s], 16)

            def load_tables(i):
                sp.dma_start(tab[:, 2 * i:2 * i + 2], tab_d[:, 2 * i:2 * i + 2]).then_inc(tab_in[i], 16)

            def spread_queries(p, s):
                sp.wait_ge(t_ev, 2 * UNITS * p + 2 * T * (s + 1))
                for h in range(HH):
                    rows = slice(h * HD, (h + 1) * HD)
                    sp.dma_start(q_wide[rows, s, :, h, :], qT[rows, s]).then_inc(wide_in[s], 16)

            def pair(p, more):
                if more:
                    for s in range(SLOTS):
                        sp.wait_ge(x1_ready, UNITS * p + T * (s + 1))
                        load_x(p + 1, s)
                        load_ctx(p + 1, s)
                    for s in range(SLOTS):
                        spread_queries(p + 1, s)
                for s in range(SLOTS):
                    sp.wait_ge(o_ev, 2 * SLOTS * p + 2 * (s + 1))
                    sp.dma_start(out_v[SLOTS * p + s], zn[:, s]).then_inc(zn_moved, 16)

            load_x(0, 0)
            load_tables(0)
            load_ctx(0, 0)
            load_tables(1)
            load_x(0, 1)
            load_ctx(0, 1)
            sp.dma_start(q_int, q_d[:, 0:8, :]).then_inc(q_in, 16)
            sp.dma_start(q_int2, q_d[:, 8:12, :]).then_inc(zn_moved, 16)
            groups = P // GROUP
            for k in range(NF):
                sp.dma_start(w_scale[:, k, :],
                             scale_d[k * groups:(k + 1) * groups].unsqueeze(1).broadcast_to([groups, GROUP, LAYERS * D])
                             ).then_inc(scale_in, 16)
            for s in range(SLOTS):
                sp.wait_ge(wide_zero, s + 1)
                spread_queries(0, s)
            with sp.Fori(0, PAIRS - 1) as p:
                pair(p, True)
            pair(PAIRS - 1, False)
            sp.wait_ge(zn_moved, 16 + 16 * SLOTS * PAIRS)

        @block.gpsimd
        def _(pool):
            def prepare_k(p, s, t):
                n = UNITS * p + T * s + t
                pool.wait_ge(ctx_in[s], 16 * p + 16)
                pool.tensor_tensor(k_prod[:, t % 2], ctx[:, s, t, :].unsqueeze(1).broadcast_to([P, 2, D]),
                                   tab[:, t, 2:4, :], ALU.mult).then_inc(k_mul, 1)
                pool.wait_ge(k_mul, n + 1)
                pairs = k_prod[:, t % 2].rearrange("p a (i r) -> p a i r", r=2)
                pool.tensor_tensor(kr[:, s, t, :].rearrange("p (i r) -> p i r", r=2), pairs[:, 0],
                                   pairs[:, 1, :, ::-1], ALU.add).then_inc(k_ready, 1)

            def gate_rows(p, s):
                pool.wait_ge(x_ve, SLOTS * p + s + 1)
                pool.tensor_tensor(xrs[:, s, :], xve[:, s, :], minus_half[:, :], ALU.pow).then_inc(x_rs, 1)
                pool.wait_ge(x_rs, SLOTS * p + s + 1)
                pool.tensor_tensor(row_gate[:, s, :], xrs[:, s, :], tanh_gate[:, 0:1].broadcast_to([P, T]),
                                   ALU.mult).then_inc(rg_ready, 1)

            def inverse_std(p, e):
                s, d = e // 2 % SLOTS, e % 2
                n = LN_EVENTS * p + e
                pool.wait_ge(ln_ve, 2 * n + 2)
                pool.tensor_tensor(rs[:, s, d], ve[:, s, d], minus_half[:, 0:2], ALU.pow).then_inc(ln_rs, 1)
                pool.wait_ge(ln_rs, n + 1)
                pool.tensor_tensor(nb[:, s, d], nm[:, s, d], rs[:, s, d], ALU.mult).then_inc(ln_nb, 1)

            def pair(p, more):
                for d in range(2):
                    inverse_std(p, ln_event(0, 0, d))
                for t in range(T - 1) if more else []:
                    prepare_k(p + 1, 0, t)
                for d in range(2):
                    inverse_std(p, ln_event(0, 1, d))
                    if more and d == 0:
                        prepare_k(p + 1, 0, T - 1)
                for blk in range(BLOCKS):
                    for s in range(SLOTS):
                        for d in range(2):
                            inverse_std(p, ln_event(blk + 1, s, d))
                        if more and (blk, s) in ((0, 1), (1, 0)):
                            for t in range(2 * blk, 2 * blk + 2):
                                prepare_k(p + 1, 1, t)
                for s in range(SLOTS) if more else []:
                    gate_rows(p + 1, s)

            pool.memset(minus_half[:, :], -0.5).then_inc(half_set, 1)
            pool.memset(ones[:, :], 1.0).then_inc(ones_set, 1)
            pool.memset(q_wide[:, 0].rearrange("p f h s -> p (f h s)"), 0.0).then_inc(wide_zero, 1)
            for s in range(SLOTS):
                for t in range(T):
                    pool.wait_ge(tab_in[t // 2], 16)
                    prepare_k(0, s, t)
            pool.wait_ge(half_set, 1)
            pool.wait_ge(gate_tanh, 1)
            for s in range(SLOTS):
                gate_rows(0, s)
            pool.memset(q_wide[:, 1].rearrange("p f h s -> p (f h s)"), 0.0).then_inc(wide_zero, 1)
            with pool.Fori(0, PAIRS - 1) as p:
                pair(p, True)
            pair(PAIRS - 1, False)

        @block.scalar
        def _(act):
            act.dma_start(const[:, :], const_d).then_inc(const_in, 16)
            act.dma_start(bias_f, bias_d.partition_broadcast(BIAS_ROWS)).then_inc(bias_in, 16)
            act.dma_start(la[0:LORA_ROWS * RANK], la_d).then_inc(lora_in, 16)
            act.dma_start(lbt[0:LORA_ROWS * RANK], lbt_d).then_inc(lora_in, 16)
            act.dma_start(gate[:, :], gates_d.partition_broadcast(P)).then_inc(gate_in, 16)
            act.dma_start(vec[:, :, :, :], vec_d).then_inc(vec_in, 16)

            def normalise(p, e, src):
                s, d = e // 2 % SLOTS, e % 2
                act.wait_ge(ln_nb, LN_EVENTS * p + e + 1)
                for i in range(2):
                    act.activation(zn[:, s, 2 * d + i, :], src(s, d, i), ACT.Identity,
                                   bias=nb[:, s, d, i:i + 1], scale=rs[:, s, d, i:i + 1]).then_inc(zn_ready, 1)

            def from_x1(s, d, i):
                return x1[:, s, 2 * d + i, :]

            def from_y1(s, d, i):
                return bank[2 * s + d][:, i * D:(i + 1) * D]

            def evacuate_intra(p, u):
                act.wait_ge(intra_ps, 2 * UNITS * p + 2 * u + 2)
                if u >= 2:
                    act.wait_ge(tok_ps, UNITS * p + u - 1)
                act.activation(intra[:, u % 2].rearrange("p g n -> p (g n)"), bank[2 + u % 2][:, 0:256],
                               ACT.Copy).then_inc(intra_ev, 1)

            def spread_values(p, s):
                act.wait_ge(ctx_in[s], 16 * p + 16)
                for c in range(NC):
                    rows = slice(c * C, (c + 1) * C)
                    act.activation(v_chunk[rows, s, :, :, c, :].rearrange("p t h e -> p (t h) e"),
                                   ctx[rows, s].rearrange("p t (h e) -> p (t h) e", e=HD),
                                   ACT.Copy).then_inc(v_ready, 1)

            def gelu(p, blk, s):
                n = (BLOCKS * p + blk) * SLOTS + s
                act.wait_ge(z_ps, n + 1)
                for f in range(NF):
                    act.activation(uT[:, s, f, :], bank[4 + 2 * s + f][:, :], ACT.Gelu,
                                   bias=vec[:, 1, blk, f:f + 1], scale=vec[:, 0, blk, f:f + 1]).then_inc(u_ready, 1)

            def evacuate_qk(p, u, src):
                s, t = u // T, u % T
                act.wait_ge(t_ps, UNITS * p + u + 1)
                halves = src[:, :].rearrange("p (a n) -> p a n", a=4)
                cols = slice(t * P, (t + 1) * P)
                act.activation(qT[:, s, :, cols], halves[:, 0:NF], ACT.Copy).then_inc(t_ev, 1)
                act.activation(kT[:, s, :, cols], halves[:, NF:2 * NF], ACT.Copy).then_inc(t_ev, 1)

            def evacuate_h(p, s, f):
                act.wait_ge(h_ps, 3 * p + (f + 1 if s == 0 else 3))
                act.activation(hT[s][:, f, :], bank[6][:, :], ACT.Copy).then_inc(h_ev_act, 1)

            def pair(p, more):
                for u in range(UNITS):
                    evacuate_intra(p, u)
                    if u == T:
                        act.wait_ge(zn_moved, 16 + 16 * SLOTS * p)
                        for d in range(2):
                            normalise(p, ln_event(0, 0, d), from_x1)
                    if T < u < T + 1 + NF:
                        evacuate_h(p, 0, u - T - 1)
                for d in range(2):
                    normalise(p, ln_event(0, 1, d), from_x1)
                normalise(p, ln_event(1, 0, 0), from_y1)
                evacuate_h(p, 1, 0)
                normalise(p, ln_event(1, 0, 1), from_y1)
                for blk in range(BLOCKS):
                    for s in range(SLOTS):
                        gelu(p, blk, s)
                        if more and s == 0 and blk >= 1:
                            spread_values(p + 1, blk - 1)
                        if (blk, s) != (BLOCKS - 1, SLOTS - 1):
                            for d in range(2):
                                normalise(p, ln_event(blk + 1 + s, 1 - s, d), from_y1)
                        if more and blk == 0:
                            for j in range(2):
                                evacuate_qk(p + 1, 2 * s + j, bank[4 + 2 * s + j])
                for u in range(T, UNITS) if more else []:
                    evacuate_qk(p + 1, u, bank[u % 2])

            act.wait_ge(const_in, 16)
            act.activation(v_chunk[:, :, :, :, :, :].rearrange("p s t h c e -> p (s t h c) e"),
                           const[:, 0:HD].unsqueeze(1).broadcast_to([P, SLOTS * T * HEADS * NC, HD]),
                           ACT.Copy, scale=0.0).then_inc(v_zero, 1)
            act.wait_ge(gate_in, 16)
            act.activation(tanh_gate[:, :], gate[:, :], ACT.Tanh).then_inc(gate_tanh, 1)
            act.wait_ge(v_zero, 1)
            spread_values(0, 0)
            for u in range(UNITS):
                evacuate_qk(0, u, bank[6 + u % 2])
                if u == T - 1:
                    act.wait_ge(q_in, 16)
                    act.wait_ge(zn_moved, 16)
                    for l in range(LAYERS):
                        src = q_int[:, 2 * l:2 * l + 2, :] if l < 4 else q_int2[:, 2 * l - 8:2 * l - 6, :]
                        act.activation(wt[:, l], src, ACT.Copy, bias=-1.0, scale=1.0 / 7.5).then_inc(w_deq, 1)
                    spread_values(0, 1)
            act.wait_ge(vec_in, 16)
            with act.Fori(0, PAIRS - 1) as p:
                pair(p, True)
            pair(PAIRS - 1, False)

        @block.vector
        def _(dve):
            def prepare_q(p, s, t):
                n = UNITS * p + T * s + t
                two = slice(t, t + 2)
                dve.wait_ge(x_in[s], 16 * p + 16)
                for i in range(t, t + 2):
                    dve.bn_stats(xstat[:, s, i, :], x[:, s, i, :]).then_inc(x_stat, 1)
                dve.wait_ge(x_stat, n + 2)
                dve.tensor_tensor(xsum[:, s, two], xstat[:, s, two, 1], xstat[:, s, two, 4],
                                  ALU.add).then_inc(x_sum, 1)
                dve.wait_ge(x_sum, UNITS // 2 * p + T // 2 * s + t // 2 + 1)
                dve.tensor_scalar(xmean[:, s, two], xsum[:, s, two], 0.5, None, ALU.mult).then_inc(x_mean, 1)
                dve.wait_ge(x_mean, UNITS // 2 * p + T // 2 * s + t // 2 + 1)
                for i in range(t, t + 2):
                    dve.scalar_tensor_tensor(q_prod[:, i % 2], x[:, s, i, :].unsqueeze(1).broadcast_to([P, 2, D]),
                                             xmean[:, s, i:i + 1], tab[:, i, 0:2, :], ALU.subtract,
                                             ALU.mult).then_inc(q_mul, 1)
                for i in range(t, t + 2):
                    dve.wait_ge(q_mul, n + i - t + 1)
                    pairs = q_prod[:, i % 2].rearrange("p a (i r) -> p a i r", r=2)
                    dve.tensor_tensor(qr[:, s, i, :].rearrange("p (i r) -> p i r", r=2), pairs[:, 0],
                                      pairs[:, 1, :, ::-1], ALU.add).then_inc(q_ready, 1)
                if t == T - 2:
                    m = SLOTS * p + s
                    dve.tensor_tensor(xdiff[:, s, :], xstat[:, s, :, 1], xstat[:, s, :, 4],
                                      ALU.subtract).then_inc(x_var, 1)
                    dve.scalar_tensor_tensor(xm2[:, s, :], xstat[:, s, :, 2], D * LN_EPS, xstat[:, s, :, 5],
                                             ALU.add, ALU.add).then_inc(x_var, 1)
                    dve.wait_ge(x_var, 3 * m + 2)
                    dve.scalar_tensor_tensor(xd2[:, s, :], xdiff[:, s, :], 0.25, xdiff[:, s, :],
                                             ALU.mult, ALU.mult).then_inc(x_var, 1)
                    dve.wait_ge(x_var, 3 * m + 3)
                    dve.scalar_tensor_tensor(xve[:, s, :], xm2[:, s, :], 1.0 / D, xd2[:, s, :],
                                             ALU.mult, ALU.add).then_inc(x_ve, 1)

            def statistics(p, e, src, todo=range(2)):
                s, d = e // 2 % SLOTS, e % 2
                m = LN_EVENTS * p + e
                n = 2 * m
                for i in todo:
                    dve.bn_stats(st[:, s, d, i, :], src(s, d, i)).then_inc(ln_st, 1)
                if 1 not in todo:
                    return
                dve.wait_ge(ln_st, n + 2)
                dve.scalar_tensor_tensor(nm2[:, s, d], st[:, s, d, :, 1], -1.0, st[:, s, d, :, 4],
                                         ALU.mult, ALU.subtract).then_inc(ln_mv, 1)
                for i in range(2):
                    dve.bn_aggr(mv[:, s, d, i, :], st[:, s, d, i, :]).then_inc(ln_mv, 1)
                dve.wait_ge(ln_mv, 3 * m + 3)
                dve.tensor_scalar(ve[:, s, d], mv[:, s, d, :, 1], LN_EPS, None, ALU.add).then_inc(ln_ve, 1)
                dve.tensor_scalar(nm[:, s, d], nm2[:, s, d], 0.5, None, ALU.mult).then_inc(ln_ve, 1)

            def x1_statistics(p, s, d, todo=range(2)):
                dve.wait_ge(x1_ready, UNITS * p + T * s + 2 * d + todo[-1] + 1)
                statistics(p, ln_event(0, s, d), lambda s, d, i: x1[:, s, 2 * d + i, :], todo)

            def y1_statistics(p, blk, s):
                for d in range(2):
                    dve.wait_ge(y1_ps, ((BLOCKS * p + blk) * SLOTS + s) * 2 + d + 1)
                    statistics(p, ln_event(blk + 1, s, d), lambda s, d, i: bank[2 * s + d][:, i * D:(i + 1) * D])

            def evacuate_scores(p, i):
                dve.wait_ge(score_ps, 2 * UNITS * p + i + 1)
                if i >= 2:
                    dve.wait_ge(intra_ps, 2 * UNITS * p + i - 1)
                dve.tensor_tensor(sT[:, i % 2], bank[i % 2][:, :].rearrange("p (h n) -> p h n", h=HH),
                                  causal.unsqueeze(1).broadcast_to([P, HH, C]), ALU.mult).then_inc(score_ev, 1)

            def evacuate_state(p, s, k):
                n = (NC * T - 1) * (SLOTS * p + s) + k
                dve.wait_ge(state_ps, n + 1)
                u_read = T * s + (k - 3) // NC
                if k >= 3:
                    dve.wait_ge(tok_ps, UNITS * p + u_read + 1)
                quarters = [P, NF, P // PAIR_W, PAIR_W]
                dve.tensor_tensor(
                    state[:, s, (k + 1) % 4].rearrange("p f (j n) -> p f j n", n=PAIR_W),
                    bank[6 + s][:, 0:NF * PAIR_W].rearrange("p (f n) -> p f n", f=NF).unsqueeze(2).broadcast_to(quarters),
                    diag16.rearrange("p (j n) -> p j n", n=PAIR_W).unsqueeze(1).broadcast_to(quarters),
                    ALU.mult).then_inc(state_ev, 1)

            def residual_x1(p, u):
                s, t = u // T, u % T
                dve.wait_ge(tok_ps, UNITS * p + u + 1)
                dve.scalar_tensor_tensor(x1[:, s, t, :], bank[4 + u % 2][:, 0:256], row_gate[:, s, t:t + 1],
                                         x[:, s, t, :], ALU.mult, ALU.add).then_inc(x1_ready, 1)

            def evacuate_h(p):
                dve.wait_ge(h_ps, 3 * p + 3)
                dve.tensor_copy(hT[1][:, 1, :], bank[7][:, :]).then_inc(h_ev_dve, 1)

            def residual_h(p, blk, s):
                n = (BLOCKS * p + blk) * SLOTS + s
                for f in range(NF):
                    dve.wait_ge(y2_ps, NF * n + f + 1)
                    dve.scalar_tensor_tensor(hT[s][:, f, :], bank[2 * s + f][:, :], vec[:, 2, blk, f:f + 1],
                                             hT[s][:, f, :], ALU.add, ALU.add).then_inc(h_res, 1)

            def output(p, s):
                for d in range(2):
                    dve.wait_ge(o_ps, (SLOTS * p + s) * 2 + d + 1)
                    dve.scalar_tensor_tensor(zn[:, s, 2 * d:2 * d + 2, :].rearrange("p t d -> p (t d)"),
                                             bank[4 + 2 * s + d][:, :], tanh_gate[:, 1:2],
                                             x1[:, s, 2 * d:2 * d + 2, :].rearrange("p t d -> p (t d)"),
                                             ALU.mult, ALU.add).then_inc(o_ev, 1)

            def pair(p, more):
                dve.wait_ge(rg_ready, SLOTS * (p + 1))
                for i in range(2 * UNITS):
                    u, f = i // 2, i % 2
                    evacuate_scores(p, i)
                    if i >= 1 and (i - 1) % (NC * T) < NC * T - 1:
                        evacuate_state(p, (i - 1) // (NC * T), (i - 1) % (NC * T))
                    if f == 1 and u >= 1:
                        residual_x1(p, u - 1)
                        if u % 2 == 0:
                            x1_statistics(p, (u - 1) // T, (u - 1) % T // 2)
                x1_statistics(p, 1, 1, range(0, 1))
                residual_x1(p, UNITS - 1)
                x1_statistics(p, 1, 1, range(1, 2))
                y1_statistics(p, 0, 0)
                evacuate_h(p)
                for blk in range(BLOCKS):
                    if more:
                        prepare_q(p + 1, *((0, 0), (1, 0), (1, 2))[blk])
                    y1_statistics(p, blk, 1)
                    residual_h(p, blk, 0)
                    if more and blk == 0:
                        prepare_q(p + 1, 0, 2)
                    if blk + 1 < BLOCKS:
                        y1_statistics(p, blk + 1, 0)
                    else:
                        output(p, 0)
                    residual_h(p, blk, 1)
                output(p, 1)

            dve.memset(bias_rows[:, :, :].rearrange("p b d -> p (b d)"), 0.0).then_inc(bias_set, 1)
            dve.wait_ge(bias_in, 16)
            dve.wait_ge(bias_set, 1)
            for j in range(3):
                dve.tensor_copy(bias_h[:, :, :], bias_f).then_inc(bias_split, 1)
                dve.wait_ge(bias_split, 2 * j + 1)
                dve.tensor_copy(bias_rows[32 * j:32 * j + 1], bias_h[32 * j:32 * j + 1]).then_inc(bias_set, 1)
                if j < 2:
                    dve.tensor_tensor(bias_f, bias_f, bias_h[:, :, :], ALU.subtract).then_inc(bias_split, 1)
                    dve.wait_ge(bias_split, 2 * j + 2)
                    dve.wait_ge(bias_set, j + 2)
            for s in range(SLOTS):
                for t in range(0, T, 2):
                    dve.wait_ge(tab_in[t // 2], 16)
                    prepare_q(0, s, t)
            dve.wait_ge(scale_in, 16 * NF)
            for l in range(LAYERS):
                dve.wait_ge(w_deq, l + 1)
                dve.tensor_tensor(wt[:, l], wt[:, l], w_scale[:, :, l * D:(l + 1) * D], ALU.mult).then_inc(w_scaled, 1)
            for l in range(LAYERS):
                dve.wait_ge(w_scaled, l + 1)
                dve.wait_ge(lora_ps, l + 1)
                dve.tensor_tensor(wt[:, l].rearrange("p k o -> p (k o)"), bank[l][:, :],
                                  wt[:, l].rearrange("p k o -> p (k o)"), ALU.add).then_inc(w_ready, 1)
            dve.wait_ge(gate_tanh, 1)
            dve.wait_ge(const_in, 16)
            dve.wait_ge(vec_in, 16)
            with dve.Fori(0, PAIRS - 1) as p:
                pair(p, True)
            pair(PAIRS - 1, False)

        @block.tensor
        def _(pe):
            def transpose_qk(p, u, dst):
                s, t = u // T, u % T
                pe.wait_ge(q_ready, UNITS * p + u + 1)
                pe.wait_ge(k_ready, UNITS * p + u + 1)
                for a, src in enumerate((qr, kr)):
                    for f in range(NF):
                        col = (a * NF + f) * P
                        last = pe.transpose(dst[:, col:col + P], src[:, s, t, f * P:(f + 1) * P], ident)
                last.then_inc(t_ps, 1)

            def scores(p, i):
                u, f = i // 2, i % 2
                s, t = u // T, u % T
                if u % T == 0 and f == 0:
                    pe.wait_ge(wide_in[s], 16 * HH * (p + 1))
                    pe.wait_ge(t_ev, 2 * UNITS * (p + 1))
                    pe.wait_ge(v_ready, NC * (SLOTS * p + s + 1))
                    pe.wait_ge(ctx_in[s], 16 * (p + 1))
                if i >= 2:
                    pe.wait_ge(score_ev, 2 * UNITS * p + i - 1)
                for c in range(NC):
                    cols = slice(t * P + c * C, t * P + (c + 1) * C)
                    last = pe.matmul(bank[i % 2][c * C:(c + 1) * C, :], kT[:, s, f, cols], q_wide[:, s, f, :, cols],
                                     start=True, stop=True)
                last.then_inc(score_ps, 1)

            def update_state(p, s, k):
                t, c = k // NC, k % NC
                n = (NC * T - 1) * (SLOTS * p + s) + k
                if k >= 1:
                    pe.wait_ge(state_ev, n)
                elif s == 0:
                    pe.wait_ge(t_ev, 2 * UNITS * (p + 1))
                for f in range(NF):
                    for j in range(P // PAIR_W):
                        heads = slice(HH * f + 2 * j, HH * f + 2 * j + 2)
                        cols = slice(PAIR_W * j, PAIR_W * (j + 1))
                        last = pe.matmul(bank[6 + s][cols, f * PAIR_W:(f + 1) * PAIR_W],
                                         kr[:, s, t, f * P + PAIR_W * j:f * P + PAIR_W * (j + 1)],
                                         v_chunk[:, s, t, heads, c, :],
                                         start=(k == 0 and f == 0), stop=(k == NC * T - 2), skip_group_check=True)
                last.then_inc(state_ps, 1)

            def intra_chunk(p, i):
                u, f = i // 2, i % 2
                s, t = u // T, u % T
                pe.wait_ge(score_ev, 2 * UNITS * p + i + 1)
                if f == 0 and u >= 2:
                    pe.wait_ge(intra_ev, UNITS * p + u - 1)
                for h in range(HH):
                    head = HH * f + h
                    j, g = head % 4, head // 4
                    last = pe.matmul(bank[2 + u % 2][32 * j:32 * (j + 1), g * C:(g + 1) * C],
                                     v_chunk[:, s, t, head].rearrange("p c e -> p (c e)"), sT[:, i % 2, h, :],
                                     start=True, stop=True)
                last.then_inc(intra_ps, 1)

            def to_tokens(p, u):
                s, t = u // T, u % T
                pe.wait_ge(intra_ev, UNITS * p + u + 1)
                if u >= 2:
                    pe.wait_ge(x1_ready, UNITS * p + u - 1)
                k = min(NC * t, NC * T - 2)
                pe.wait_ge(state_ev, (NC * T - 1) * (SLOTS * p + s) + k + 1)
                out = bank[4 + u % 2]
                for c in range(NC):
                    chunk = NC * t + c
                    rows = slice(c * C, (c + 1) * C)
                    first = True
                    if chunk > 0:
                        for f in range(NF):
                            pe.matmul(out[rows, f * P:(f + 1) * P], qT[:, s, f, chunk * C:(chunk + 1) * C],
                                      state[:, s, chunk % 4, f, :], start=first, stop=False, skip_group_check=True)
                            first = False
                    for g in range(HEADS // 4):
                        last = pe.matmul(out[rows, g * C:(g + 1) * C], intra[:, u % 2, g, :], pick[:, c, :],
                                         start=first, stop=True, skip_group_check=True)
                        first = False
                last.then_inc(tok_ps, 1)

            def transpose_half(dst, s, f):
                for t in range(T):
                    last = pe.transpose(dst[:, t * P:(t + 1) * P], zn[:, s, t, f * P:(f + 1) * P], ident)
                return last

            def h_to_features(p):
                pe.wait_ge(zn_ready, 2 * LN_EVENTS * p + 2 * ln_event(0, 1, 1) + 2)
                pe.wait_ge(h_ev_act, 3 * p + NF)
                for f in range(NF):
                    last = transpose_half(bank[6 + f], 1, f)
                last.then_inc(h_ps, 1)

            def h_half_to_features(p, f):
                if f == 0:
                    pe.wait_ge(zn_ready, 2 * LN_EVENTS * p + 2 * ln_event(0, 0, 1) + 2)
                else:
                    pe.wait_ge(h_ev_act, 3 * p + f)
                transpose_half(bank[6], 0, f).then_inc(h_ps, 1)

            def linear1(p, blk, s, tiles=range(T)):
                n = (BLOCKS * p + blk) * SLOTS + s
                if blk == 0:
                    pe.wait_ge(h_ev_act, 3 * p + NF + s)
                    if s == 1:
                        pe.wait_ge(h_ev_dve, p + 1)
                else:
                    pe.wait_ge(h_res, NF * (n - SLOTS) + NF)
                for t in tiles:
                    out = bank[2 * s + t // 2][:, (t % 2) * D:(t % 2 + 1) * D]
                    for f in range(NF):
                        pe.matmul(out, hT[s][:, f, t * P:(t + 1) * P], wt[:, 2 * blk, f, :], start=(f == 0), stop=False)
                    last = pe.matmul(out, ones[:, :], bias_rows[:, blk, :], start=False, stop=True)
                    if t % 2 == 1:
                        last.then_inc(y1_ps, 1)

            def z_to_features(p, blk, s, more):
                pe.wait_ge(zn_ready, 2 * LN_EVENTS * p + 2 * ln_event(blk + 1, s, 1) + 2)
                if more and blk == 1:
                    pe.wait_ge(t_ev, 2 * UNITS * (p + 1) + 4 * s + 4)
                for f in range(NF):
                    last = transpose_half(bank[4 + 2 * s + f], s, f)
                last.then_inc(z_ps, 1)

            def linear2(p, blk, s):
                n = (BLOCKS * p + blk) * SLOTS + s
                pe.wait_ge(u_ready, NF * n + NF)
                for f in range(NF):
                    for k in range(NF):
                        last = pe.matmul(bank[2 * s + f][:, :], wt[:, 2 * blk + 1, k, f * P:(f + 1) * P],
                                         uT[:, s, k, :], start=(k == 0), stop=(k == NF - 1))
                    last.then_inc(y2_ps, 1)

            def h_to_tokens(p, s):
                n = (BLOCKS * p + BLOCKS - 1) * SLOTS + s
                pe.wait_ge(h_res, NF * n + NF)
                for t in range(T):
                    for f in range(NF):
                        col = (t % 2) * D + f * P
                        last = pe.transpose(bank[4 + 2 * s + t // 2][:, col:col + P],
                                            hT[s][:, f, t * P:(t + 1) * P], ident)
                    if t % 2 == 1:
                        last.then_inc(o_ps, 1)

            def transpose_next(p, s, free, turn):
                for j in range(2):
                    u = T * s + 2 * turn + j
                    if s == 1 and turn == 1:
                        pe.wait_ge(t_ev, 2 * UNITS * (p + 1) + 2 * (u - 2) + 2)
                    transpose_qk(p + 1, u, bank[free + j])

            def pair(p, more):
                for i in range(2 * UNITS):
                    u, f = i // 2, i % 2
                    scores(p, i)
                    if i >= 1:
                        intra_chunk(p, i - 1)
                        if (i - 1) % (NC * T) < NC * T - 1:
                            update_state(p, (i - 1) // (NC * T), (i - 1) % (NC * T))
                    if f == 0 and T + 2 <= u < T + 2 + NF:
                        h_half_to_features(p, u - T - 2)
                    if f == 1 and u >= 1:
                        to_tokens(p, u - 1)
                intra_chunk(p, 2 * UNITS - 1)
                linear1(p, 0, 0, range(0, 1))
                to_tokens(p, UNITS - 1)

                linear1(p, 0, 0, range(1, T))
                h_to_features(p)
                for blk in range(BLOCKS):
                    if blk == 0:
                        linear1(p, 0, 1, range(0, 2))
                        z_to_features(p, 0, 0, more)
                        linear1(p, 0, 1, range(2, T))
                    else:
                        z_to_features(p, blk, 0, more)
                        linear1(p, blk, 1)
                    linear2(p, blk, 0)
                    if more and blk == 0:
                        transpose_next(p, 0, 4, 0)
                    z_to_features(p, blk, 1, more)
                    if blk + 1 < BLOCKS:
                        linear1(p, blk + 1, 0)
                    else:
                        h_to_tokens(p, 0)
                        if more:
                            transpose_next(p, 1, 0, 0)
                    linear2(p, blk, 1)
                    if more and blk == 0:
                        transpose_next(p, 0, 6, 1)
                if more:
                    transpose_next(p, 1, 0, 1)
                h_to_tokens(p, 1)

            def lora_product(l):
                rows = slice(RANK * (l % LORA_ROWS), RANK * (l % LORA_ROWS + 1))
                for k in range(NF):
                    last = pe.matmul(bank[l][:, k * D:(k + 1) * D], la[rows, l // LORA_ROWS, k * P:(k + 1) * P],
                                     lbt[rows, l // LORA_ROWS, :], start=True, stop=True)
                last.then_inc(lora_ps, 1)

            pe.wait_ge(const_in, 16)
            pe.wait_ge(lora_in, 32)
            for u in range(UNITS):
                if u >= 2:
                    pe.wait_ge(t_ev, 2 * u - 2)
                transpose_qk(0, u, bank[6 + u % 2])
                if u == 1 or u == 3:
                    for l in range(LAYERS // 2 * (u // 2), LAYERS // 2 * (u // 2 + 1)):
                        lora_product(l)
            pe.wait_ge(w_ready, LAYERS)
            pe.wait_ge(bias_set, 4)
            pe.wait_ge(ones_set, 1)
            with pe.Fori(0, PAIRS - 1) as p:
                pair(p, True)
            pair(PAIRS - 1, False)


def constants():
    f = np.float32
    lin = np.linspace(np.log(1.0 / 32.0), np.log(1.0 / 512.0), HEADS).astype(f)
    gamma = (f(1.0) - np.exp(lin)).astype(f).astype(np.float64)
    pos = np.arange(S, dtype=f)
    base = ((np.arange(0, HD, 2, dtype=f) + f(0.4 * HD)) / f(1.4 * HD)).astype(np.float64)
    scale = base[None, :] ** (pos.astype(np.float64) / 512.0)[:, None]
    inv_freq = (1.0 / 10000.0 ** (np.arange(HD // 2, dtype=f) / f(HD // 2))).astype(f)
    angle = (pos[:, None] * inv_freq[None, :]).astype(f).astype(np.float64)
    decay = gamma[None, :] ** (pos.astype(np.float64) - S // 2)[:, None]

    def table(trig, sign, scl, dec):
        return dec[:, :, None, None] * (trig * scl)[:, None, :, None] * np.array(sign)[None, None, None, :]

    tabs = [table(np.cos(angle), [1, 1], scale, decay), table(np.sin(angle), [1, -1], scale, decay),
            table(np.cos(angle), [1, 1], 1 / scale, 1 / decay), table(np.sin(angle), [1, -1], 1 / scale, 1 / decay)]
    tab = np.stack([a.reshape(T, P, D) for a in tabs], axis=2).transpose(1, 0, 2, 3)
    i = np.arange(P)
    const = np.zeros((P, C_END), f)
    const[:, C_ID:C_ID + P] = np.eye(P)
    const[:, C_DIAG:C_DIAG + P] = i[:, None] // HD == i[None, :] // HD
    for c in range(NC):
        for j in range(4):
            for e in range(HD):
                const[32 * j + HD * c + e, C_PICK + c * C + HD * j + e] = 1
    const[:, C_CAUSAL:C_CAUSAL + C] = np.arange(C)[None, :] >= i[:, None] % C
    return const, np.ascontiguousarray(tab.astype(f))


def kernel(x, ctx_1024, g_xattn, g_ffn, L0_ffn_qweights, L0_ffn_scales, L0_ffn_biases, L0_ffn_lora_a, L0_ffn_lora_b,
           L0_ffn_ln_gamma, L0_ffn_ln_beta):
    import concourse.bacc as bacc
    from concourse.bass_utils import run_bass_kernel_spmd

    def c(a):
        return np.ascontiguousarray(a)

    def rows_below(a):
        return c(a.reshape(-1, LORA_ROWS, RANK, D).transpose(1, 2, 0, 3).reshape(LORA_ROWS * RANK, -1, D))

    const, tab = constants()
    q, biases = np.asarray(L0_ffn_qweights), np.asarray(L0_ffn_biases)
    vec = np.stack([np.asarray(L0_ffn_ln_gamma), np.asarray(L0_ffn_ln_beta), biases[1::2]])
    arrays = {
        "x": c(x), "ctx": c(ctx_1024),
        "gates": c(np.concatenate([np.asarray(g_xattn), np.asarray(g_ffn)])),
        "qweights": c(q.transpose(2, 0, 1).reshape(NF, P, LAYERS, D).transpose(1, 2, 0, 3).reshape(P, LAYERS * NF, D)),
        "scales": c(np.asarray(L0_ffn_scales).transpose(2, 0, 1).reshape(D // GROUP, LAYERS * D)),
        "bias1": c(biases[0::2]),
        "lora_a": rows_below(np.asarray(L0_ffn_lora_a)),
        "lora_bt": rows_below(np.asarray(L0_ffn_lora_b).transpose(0, 2, 1)),
        "vectors": c(vec.reshape(3, BLOCKS, NF, P).transpose(3, 0, 1, 2)),
        "const": const, "tables": tab,
    }
    nc = bacc.Bacc("TRN2", target_bir_lowering=False, num_devices=1)
    args = [nc.dram_tensor(f"in_{k}", a.shape, mybir.dt.from_np(a.dtype), kind="ExternalInput").ap()
            for k, a in arrays.items()]
    out = nc.dram_tensor("out", (B, S, D), F32, kind="ExternalOutput").ap()
    build(nc, *args, out)
    r = run_bass_kernel_spmd(nc, [{f"in_{k}": a for k, a in arrays.items()}], core_ids=[0])
    return r.results[0]["out"]
```

```python
from contextlib import ExitStack

import numpy as np

import concourse.bass as bass
from concourse import mybir
from concourse.alu_op_type import AluOpType as ALU

F32 = mybir.dt.float32
BF16 = mybir.dt.bfloat16
I32 = mybir.dt.int32
F32R = mybir.dt.float32r
ACT = mybir.ActivationFunctionType

B, S, D = 8, 512, 256
HEADS, HD = 16, 16
P = 128
T = S // P
NF = D // P
C = 64
NC = P // C
HH = HEADS // NF
SLOTS = 2
PAIRS = B // SLOTS
UNITS = SLOTS * T
PAIR_W = 2 * HD
BLOCKS = 3
LORA_ROWS = 3
LAYERS = 2 * BLOCKS
RANK = 32
GROUP = 16
QUERY_TILES = 4
BIAS_ROWS = 65
LN_EPS = 1e-5
LN_PASSES = BLOCKS + 1

C_ID, C_DIAG, C_PICK, C_CAUSAL, C_END = 0, P, 2 * P, 3 * P, 3 * P + C


def build(nc, x_d, ctx_d, gates_d, q_d, scale_d, bias_d, la_d, lbt_d, vec_d, const_d, tab_d, out_d):
    es = ExitStack()
    with es:
        def sb(name, shape, dt=F32):
            return es.enter_context(nc.sbuf_tensor(name, shape, dt))

        def before(name, shape):
            with nc.sbuf_tensor(name, shape, F32) as t:
                return t

        def sem(name):
            return es.enter_context(nc.semaphore(name))

        def per_slot(name):
            return [sem(f"{name}{s}") for s in range(SLOTS)]

        const = sb("const", [P, C_END])
        ident = const[:, C_ID:C_ID + P]
        diag16 = const[:, C_DIAG:C_DIAG + P]
        pick = const[:, C_PICK:C_PICK + P].rearrange("p (c n) -> p c n", c=NC)
        causal = const[:, C_CAUSAL:C_CAUSAL + C]
        tab = sb("tab", [P, T, 4, D])
        vec = sb("vec", [P, 3, BLOCKS, NF])
        gate = sb("gate", [P, 2])
        tanh_gate = sb("tanh_gate", [P, 2])
        minus_half = sb("minus_half", [P, T])
        w1 = sb("w1", [P, BLOCKS, NF, D])
        w2_hi = sb("w2_hi", [P, BLOCKS, NF, D], F32R)
        w2 = before("w2", [P, BLOCKS, NF, D])
        w2_lo = sb("w2_lo", [P, BLOCKS, NF, D], F32R)

        def weight(l):
            return w1[:, l // 2] if l % 2 == 0 else w2[:, l // 2]
        ones = sb("ones", [P, P], BF16)
        bias_rows = sb("bias_rows", [P, BLOCKS, D], BF16)
        x = sb("x", [P, SLOTS, T, D])
        ctx = sb("ctx", [P, SLOTS, T, D])
        v_chunk = sb("v_chunk", [P, SLOTS, T, HEADS, NC, HD])
        qr = sb("qr", [P, QUERY_TILES, D])
        kr = sb("kr", [P, SLOTS, T, D])
        q_prod = sb("q_prod", [P, 2, 2, D])
        k_prod = sb("k_prod", [P, 2, 2, D])
        qT = sb("qT", [P, SLOTS, NF, S])
        kT = sb("kT", [P, SLOTS, NF, S])
        q_wide = sb("q_wide", [P, SLOTS, NF, HH, S])
        u_exact = sb("u_exact", [P, NF, S])
        bias_h = u_exact[0:BIAS_ROWS].rearrange("p f n -> p (f n)")[:, 0:BLOCKS * D // 2].bitcast(BF16).rearrange(
            "p (b d) -> p b d", b=BLOCKS)
        intra = u_exact[:, 0].rearrange("p (b g n) -> p b g n", b=2, g=HEADS // 4)
        xstat = sb("xstat", [P, SLOTS, T, 6])
        xsum, minus_mean, xdiff = sb("xsum", [P, SLOTS, T]), sb("minus_mean", [P, SLOTS, T]), sb("xdiff", [P, SLOTS, T])
        xm2, xd2 = sb("xm2", [P, SLOTS, T]), sb("xd2", [P, SLOTS, T])
        xve = sb("xve", [P, SLOTS, T])
        row_gate = sb("row_gate", [P, SLOTS, T])
        xrs = sb("xrs", [P, SLOTS, T])
        st = sb("st", [P, SLOTS, 2, 2, 6])
        mv = sb("mv", [P, SLOTS, 2, 2, 2])
        ve = sb("ve", [P, SLOTS, 2, 2])
        nm = sb("nm", [P, SLOTS, 2, 2])
        nm2 = sb("nm2", [P, SLOTS, 2, 2])
        rs = sb("rs", [P, SLOTS, 2, 2])
        nb = sb("nb", [P, SLOTS, 2, 2])
        x1 = sb("x1", [P, SLOTS, T, D])
        zn = sb("zn", [P, SLOTS, T, D])
        shared = before("shared", [P, 4 * NF * S])
        state = shared[:, 0:2 * NF * S].rearrange("p (s r f n) -> p s r f n", s=SLOTS, r=4, f=NF)
        sT = shared[:, 2 * NF * S:3 * NF * S].rearrange("p (b h n) -> p b h n", b=2, h=HH)
        u_hi, u_lo = sb("u_hi", [P, NF, S], F32R), sb("u_lo", [P, NF, S], F32R)
        hT = [sb(f"h{s}", [P, NF, S]) for s in range(SLOTS - 1, -1, -1)][::-1]
        q_int = x1[:, :, :, :].rearrange("p s t d -> p (s t) d").bitcast(I32)
        q_int2 = zn[:, 0, :, :].bitcast(I32)
        bias_f = zn[0:BIAS_ROWS, 1, 0:BLOCKS, :]
        w_scale = shared[:, 0:NF * LAYERS * D].rearrange("p (k o) -> p k o", k=NF)
        la = shared[:, LAYERS * NF * D:(LAYERS * NF + 2) * D].rearrange("p (j o) -> p j o", j=2)
        lbt = shared[:, (LAYERS * NF + 2) * D:(LAYERS * NF + 4) * D].rearrange("p (j o) -> p j o", j=2)

        bank = [es.enter_context(nc.psum_tensor(f"bank{i}", [P, 512], F32)) for i in range(8)]

        const_in, vec_in, gate_in = sem("const_in"), sem("vec_in"), sem("gate_in")
        tab_in = [sem(f"tab_in{i}") for i in range(T // 2)]
        q_in, lora_in, bias_in = sem("q_in"), sem("lora_in"), sem("bias_in")
        scale_in = [sem(f"scale_in{k}") for k in range(NF)]
        x_in, ctx_in, wide_in = per_slot("x_in"), per_slot("ctx_in"), per_slot("wide_in")
        zn_moved = sem("zn_moved")
        v_zero, v_ready, wide_zero, ones_set, half_set = sem("v_zero"), sem("v_ready"), sem("wide_zero"), sem("ones_set"), sem("half_set")
        gate_tanh = sem("gate_tanh")
        bias_rounded, bias_rest, bias_set = sem("bias_rounded"), sem("bias_rest"), sem("bias_set")
        w_deq, w_scaled, lora_ps, w_ready = sem("w_deq"), sem("w_scaled"), sem("lora_ps"), sem("w_ready")
        x_stat, x_sum, x_mean, x_var = sem("x_stat"), sem("x_sum"), sem("x_mean"), sem("x_var")
        x_ve, x_rs, rg_ready = sem("x_ve"), sem("x_rs"), sem("rg_ready")
        q_mul, q_ready, k_mul, k_ready = sem("q_mul"), sem("q_ready"), sem("k_mul"), sem("k_ready")
        q_centred = sem("q_centred")
        t_ps, t_ev = sem("t_ps"), sem("t_ev")
        score_ps, score_ev = sem("score_ps"), sem("score_ev")
        state_ps, state_ev = sem("state_ps"), sem("state_ev")
        intra_ps, intra_ev = sem("intra_ps"), sem("intra_ev")
        tok_ps, x1_ready = sem("tok_ps"), sem("x1_ready")
        ln_st, ln_mv, ln_ve, ln_rs, ln_nb = sem("ln_st"), sem("ln_mv"), sem("ln_ve"), sem("ln_rs"), sem("ln_nb")
        zn_ready = sem("zn_ready")
        h_ps, h_ev_act, h_ev_dve = sem("h_ps"), sem("h_ev_act"), sem("h_ev_dve")
        y1_ps, z_ps, y2_ps, h_res = sem("y1_ps"), sem("z_ps"), sem("y2_ps"), sem("h_res")
        u_gelu = sem("u_gelu")
        u_lo_ready = [sem(f"u_lo_ready{f}") for f in range(NF)]
        w2_round, w2_rest = sem("w2_round"), sem("w2_rest")
        o_ps, o_ev = sem("o_ps"), sem("o_ev")

        x_v = x_d.rearrange("b (t p) d -> b p t d", p=P)
        ctx_v = ctx_d.rearrange("b (t p) d -> b p t d", p=P)
        out_v = out_d.rearrange("b (t p) d -> b p t d", p=P)

        def ln_event(k, s, d):
            return (k * SLOTS + s) * 2 + d

        LN_EVENTS = LN_PASSES * SLOTS * 2

        block = es.enter_context(nc.Block())

        @block.sync
        def _(sp):
            def load_x(p, s):
                sp.dma_start(x[:, s], x_v[SLOTS * p + s]).then_inc(x_in[s], 16)

            def load_ctx(p, s):
                sp.dma_start(ctx[:, s], ctx_v[SLOTS * p + s]).then_inc(ctx_in[s], 16)

            def load_tables(i):
                sp.dma_start(tab[:, 2 * i:2 * i + 2], tab_d[:, 2 * i:2 * i + 2]).then_inc(tab_in[i], 16)

            def spread_queries(p, s):
                sp.wait_ge(t_ev, 2 * UNITS * p + 2 * T * (s + 1))
                for h in range(HH):
                    rows = slice(h * HD, (h + 1) * HD)
                    sp.dma_start(q_wide[rows, s, :, h, :], qT[rows, s]).then_inc(wide_in[s], 16)

            def pair(p, more):
                if more:
                    for s in range(SLOTS):
                        sp.wait_ge(x1_ready, UNITS * p + T * (s + 1))
                        load_x(p + 1, s)
                        load_ctx(p + 1, s)
                    for s in range(SLOTS):
                        spread_queries(p + 1, s)
                for s in range(SLOTS):
                    sp.wait_ge(o_ev, 2 * SLOTS * p + 2 * (s + 1))
                    sp.dma_start(out_v[SLOTS * p + s], zn[:, s]).then_inc(zn_moved, 16)

            load_x(0, 0)
            load_tables(0)
            load_ctx(0, 0)
            load_tables(1)
            load_x(0, 1)
            load_ctx(0, 1)
            sp.dma_start(q_int, q_d[:, 0:8, :]).then_inc(q_in, 16)
            sp.dma_start(q_int2, q_d[:, 8:12, :]).then_inc(zn_moved, 16)
            groups = P // GROUP
            for k in range(NF):
                sp.dma_start(w_scale[:, k, :],
                             scale_d[k * groups:(k + 1) * groups].unsqueeze(1).broadcast_to([groups, GROUP, LAYERS * D])
                             ).then_inc(scale_in[k], 16)
            for s in range(SLOTS):
                sp.wait_ge(wide_zero, s + 1)
                spread_queries(0, s)
            with sp.Fori(0, PAIRS - 1) as p:
                pair(p, True)
            pair(PAIRS - 1, False)
            sp.wait_ge(zn_moved, 16 + 16 * SLOTS * PAIRS)

        @block.gpsimd
        def _(pool):
            def prepare_k(p, s, t):
                n = UNITS * p + T * s + t
                pool.wait_ge(ctx_in[s], 16 * p + 16)
                pool.tensor_tensor(k_prod[:, t % 2], ctx[:, s, t, :].unsqueeze(1).broadcast_to([P, 2, D]),
                                   tab[:, t, 2:4, :], ALU.mult).then_inc(k_mul, 1)
                pool.wait_ge(k_mul, n + 1)
                pairs = k_prod[:, t % 2].rearrange("p a (i r) -> p a i r", r=2)
                pool.tensor_tensor(kr[:, s, t, :].rearrange("p (i r) -> p i r", r=2), pairs[:, 0],
                                   pairs[:, 1, :, ::-1], ALU.add).then_inc(k_ready, 1)

            def prepare_q(p, s, t):
                n = UNITS * p + T * s + t
                u = T * s + t
                centred = qr[:, u % QUERY_TILES, :]
                pool.wait_ge(q_centred, n - UNITS + 1)
                pool.tensor_tensor(q_prod[:, t % 2], centred.unsqueeze(1).broadcast_to([P, 2, D]),
                                   tab[:, t, 0:2, :], ALU.mult).then_inc(q_mul, 1)
                pool.wait_ge(q_mul, n + 1)
                pairs = q_prod[:, t % 2].rearrange("p a (i r) -> p a i r", r=2)
                pool.tensor_tensor(centred.rearrange("p (i r) -> p i r", r=2), pairs[:, 0],
                                   pairs[:, 1, :, ::-1], ALU.add).then_inc(q_ready, 1)

            def gate_rows(p, s):
                pool.wait_ge(x_ve, SLOTS * p + s + 1)
                pool.tensor_tensor(xrs[:, s, :], xve[:, s, :], minus_half[:, :], ALU.pow).then_inc(x_rs, 1)
                pool.wait_ge(x_rs, SLOTS * p + s + 1)
                pool.tensor_tensor(row_gate[:, s, :], xrs[:, s, :], tanh_gate[:, 0:1].broadcast_to([P, T]),
                                   ALU.mult).then_inc(rg_ready, 1)

            def inverse_std(p, e):
                s, d = e // 2 % SLOTS, e % 2
                n = LN_EVENTS * p + e
                pool.wait_ge(ln_ve, 2 * n + 1)
                pool.tensor_tensor(rs[:, s, d], ve[:, s, d], minus_half[:, 0:2], ALU.pow).then_inc(ln_rs, 1)
                pool.wait_ge(ln_ve, 2 * n + 2)
                pool.wait_ge(ln_rs, n + 1)
                pool.tensor_tensor(nb[:, s, d], nm[:, s, d], rs[:, s, d], ALU.mult).then_inc(ln_nb, 1)

            def u_rest(p, blk, s):
                n = (BLOCKS * p + blk) * SLOTS + s
                pool.wait_ge(u_gelu, 2 * NF * n + 4)
                pool.tensor_tensor(u_lo[:, 1], u_exact[:, 1], u_hi[:, 1].bitcast(F32),
                                   ALU.subtract).then_inc(u_lo_ready[1], 1)

            def pair(p, more):
                for d in range(2):
                    inverse_std(p, ln_event(0, 0, d))
                for t in range(T - 1) if more else []:
                    prepare_k(p + 1, 0, t)
                for d in range(2):
                    inverse_std(p, ln_event(0, 1, d))
                    if more and d == 0:
                        prepare_k(p + 1, 0, T - 1)
                for blk in range(BLOCKS):
                    for s in range(SLOTS):
                        inverse_std(p, ln_event(blk + 1, s, 0))
                        if s == 1:
                            u_rest(p, blk, 0)
                        elif blk >= 1:
                            u_rest(p, blk - 1, 1)
                        inverse_std(p, ln_event(blk + 1, s, 1))
                        what, slot, t0 = ((prepare_q, 0, 0), (prepare_q, 0, 2), (prepare_k, 1, 0), (prepare_q, 1, 0),
                                          (prepare_k, 1, 2), (prepare_q, 1, 2))[SLOTS * blk + s]
                        for t in (t0, t0 + 1) if more else ():
                            what(p + 1, slot, t)
                for s in range(SLOTS) if more else []:
                    gate_rows(p + 1, s)

            def bias_less_row(j):
                pool.wait_ge(bias_set, j + 2)
                pool.tensor_tensor(bias_f, bias_f, bias_h[:, :, :], ALU.subtract).then_inc(bias_rest, 1)

            pool.memset(minus_half[:, :], -0.5).then_inc(half_set, 1)
            pool.memset(ones[:, :], 1.0).then_inc(ones_set, 1)
            pool.memset(q_wide[:, 0].rearrange("p f h s -> p (f h s)"), 0.0).then_inc(wide_zero, 1)
            for s in range(SLOTS):
                for t in range(T):
                    pool.wait_ge(tab_in[t // 2], 16)
                    prepare_k(0, s, t)
                if s == 0:
                    bias_less_row(0)
            pool.wait_ge(half_set, 1)
            pool.wait_ge(gate_tanh, 1)
            for s in range(SLOTS):
                gate_rows(0, s)
            bias_less_row(1)
            pool.memset(q_wide[:, 1].rearrange("p f h s -> p (f h s)"), 0.0).then_inc(wide_zero, 1)
            for b in range(BLOCKS):
                pool.wait_ge(w2_round, b + 1)
                pool.tensor_tensor(w2_lo[:, b], w2[:, b], w2_hi[:, b].bitcast(F32), ALU.subtract).then_inc(w2_rest, 1)
            with pool.Fori(0, PAIRS - 1) as p:
                pair(p, True)
            pair(PAIRS - 1, False)

        @block.scalar
        def _(act):
            act.dma_start(const[:, :], const_d).then_inc(const_in, 16)
            act.dma_start(bias_f, bias_d.partition_broadcast(BIAS_ROWS)).then_inc(bias_in, 16)
            act.dma_start(la[0:LORA_ROWS * RANK], la_d).then_inc(lora_in, 16)
            act.dma_start(lbt[0:LORA_ROWS * RANK], lbt_d).then_inc(lora_in, 16)
            act.dma_start(gate[:, :], gates_d.partition_broadcast(P)).then_inc(gate_in, 16)
            act.dma_start(vec[:, :, :, :], vec_d).then_inc(vec_in, 16)

            def normalise(p, e, src):
                s, d = e // 2 % SLOTS, e % 2
                act.wait_ge(ln_nb, LN_EVENTS * p + e + 1)
                for i in range(2):
                    act.activation(zn[:, s, 2 * d + i, :], src(s, d, i), ACT.Identity,
                                   bias=nb[:, s, d, i:i + 1], scale=rs[:, s, d, i:i + 1]).then_inc(zn_ready, 1)

            def from_x1(s, d, i):
                return x1[:, s, 2 * d + i, :]

            def from_y1(s, d, i):
                return bank[2 * s + d][:, i * D:(i + 1) * D]

            def evacuate_intra(p, u):
                act.wait_ge(intra_ps, 2 * UNITS * p + 2 * u + 2)
                if u >= 2:
                    act.wait_ge(tok_ps, UNITS * p + u - 1)
                act.activation(intra[:, u % 2].rearrange("p g n -> p (g n)"), bank[2 + u % 2][:, 0:256],
                               ACT.Copy).then_inc(intra_ev, 1)

            def spread_values(p, s, chunks=range(NC)):
                act.wait_ge(ctx_in[s], 16 * p + 16)
                for c in chunks:
                    rows = slice(c * C, (c + 1) * C)
                    act.activation(v_chunk[rows, s, :, :, c, :].rearrange("p t h e -> p (t h) e"),
                                   ctx[rows, s].rearrange("p t (h e) -> p (t h) e", e=HD),
                                   ACT.Copy).then_inc(v_ready, 1)

            def gelu(p, blk, s):
                n = (BLOCKS * p + blk) * SLOTS + s
                act.wait_ge(z_ps, n + 1)
                for dst in (u_hi, u_exact):
                    for f in range(NF):
                        act.activation(dst[:, f, :], bank[4 + 2 * s + f][:, :], ACT.Gelu,
                                       bias=vec[:, 1, blk, f:f + 1], scale=vec[:, 0, blk, f:f + 1]).then_inc(u_gelu, 1)

            def evacuate_qk(p, u, src):
                s, t = u // T, u % T
                act.wait_ge(t_ps, UNITS * p + u + 1)
                halves = src[:, :].rearrange("p (a n) -> p a n", a=4)
                cols = slice(t * P, (t + 1) * P)
                act.activation(qT[:, s, :, cols], halves[:, 0:NF], ACT.Copy).then_inc(t_ev, 1)
                act.activation(kT[:, s, :, cols], halves[:, NF:2 * NF], ACT.Copy).then_inc(t_ev, 1)

            def centre_queries(p, s, t):
                n = UNITS * p + T * s + t
                act.wait_ge(x_mean, UNITS // 2 * p + T // 2 * s + t // 2 + 1)
                act.wait_ge(t_ps, n + 2 - QUERY_TILES)
                for i in range(t, t + 2):
                    act.activation(qr[:, (T * s + i) % QUERY_TILES, :], x[:, s, i, :], ACT.Identity,
                                   bias=minus_mean[:, s, i:i + 1], scale=1.0).then_inc(q_centred, 1)

            def evacuate_h(p, s, f):
                act.wait_ge(h_ps, 3 * p + (f + 1 if s == 0 else 3))
                act.activation(hT[s][:, f, :], bank[6][:, :], ACT.Copy).then_inc(h_ev_act, 1)

            def pair(p, more):
                for u in range(UNITS):
                    evacuate_intra(p, u)
                    if u == T:
                        act.wait_ge(zn_moved, 16 + 16 * SLOTS * p)
                        for d in range(2):
                            normalise(p, ln_event(0, 0, d), from_x1)
                    if T < u < T + 1 + NF:
                        evacuate_h(p, 0, u - T - 1)
                normalise(p, ln_event(0, 1, 0), from_x1)
                if more:
                    centre_queries(p + 1, 0, 0)
                normalise(p, ln_event(0, 1, 1), from_x1)
                normalise(p, ln_event(1, 0, 0), from_y1)
                evacuate_h(p, 1, 0)
                normalise(p, ln_event(1, 0, 1), from_y1)
                for blk in range(BLOCKS):
                    for s in range(SLOTS):
                        e = SLOTS * blk + s
                        gelu(p, blk, s)
                        if blk + s < BLOCKS:
                            normalise(p, ln_event(blk + 1 + s, 1 - s, 0), from_y1)
                            if more and e in (0, 2, 3):
                                centre_queries(p + 1, *{0: (0, 2), 2: (1, 0), 3: (1, 2)}[e])
                            if more and e in (1, 4):
                                spread_values(p + 1, 0, range(e // 4, e // 4 + 1))
                            normalise(p, ln_event(blk + 1 + s, 1 - s, 1), from_y1)
                        if more and e in (1, 2):
                            for j in range(2):
                                evacuate_qk(p + 1, 2 * (e - 1) + j, bank[4 + 2 * s + j])
                for u in range(T, UNITS) if more else []:
                    evacuate_qk(p + 1, u, bank[u % 2])
                if more:
                    spread_values(p + 1, 1)

            act.wait_ge(const_in, 16)
            act.activation(v_chunk[:, :, :, :, :, :].rearrange("p s t h c e -> p (s t h c) e"),
                           const[:, 0:HD].unsqueeze(1).broadcast_to([P, SLOTS * T * HEADS * NC, HD]),
                           ACT.Copy, scale=0.0).then_inc(v_zero, 1)
            act.wait_ge(gate_in, 16)
            act.activation(tanh_gate[:, :], gate[:, :], ACT.Tanh).then_inc(gate_tanh, 1)
            act.wait_ge(v_zero, 1)
            spread_values(0, 0)
            def bias_part(j):
                act.activation(bias_h[:, :, :], bias_f, ACT.Copy).then_inc(bias_rounded, 1)
                act.wait_ge(bias_rounded, j + 1)
                act.activation(bias_rows[32 * j:32 * j + 1], bias_h[32 * j:32 * j + 1], ACT.Copy).then_inc(bias_set, 1)

            act.wait_ge(bias_in, 16)
            act.wait_ge(bias_set, 1)
            for u in range(UNITS):
                evacuate_qk(0, u, bank[6 + u % 2])
                if u == 1:
                    bias_part(0)
                if u == T - 1:
                    act.wait_ge(q_in, 16)
                    act.wait_ge(zn_moved, 16)
                    for l in range(LAYERS):
                        src = q_int[:, 2 * l:2 * l + 2, :] if l < 4 else q_int2[:, 2 * l - 8:2 * l - 6, :]
                        act.activation(weight(l), src, ACT.Copy, bias=-1.0, scale=1.0 / 7.5).then_inc(w_deq, 1)
                if u == T + 1:
                    act.wait_ge(bias_rest, 1)
                    bias_part(1)
            spread_values(0, 1)
            act.wait_ge(bias_rest, 2)
            bias_part(2)
            act.wait_ge(w_ready, LAYERS)
            act.wait_ge(bias_set, 4)
            for b in range(BLOCKS):
                act.activation(w2_hi[:, b], w2[:, b], ACT.Copy).then_inc(w2_round, 1)
            act.wait_ge(vec_in, 16)
            with act.Fori(0, PAIRS - 1) as p:
                pair(p, True)
            pair(PAIRS - 1, False)

        @block.vector
        def _(dve):
            def x_statistics(p, s, t):
                n = UNITS * p + T * s + t
                m = UNITS // 2 * p + T // 2 * s + t // 2
                two = slice(t, t + 2)
                dve.wait_ge(x_in[s], 16 * p + 16)
                for i in range(t, t + 2):
                    dve.bn_stats(xstat[:, s, i, :], x[:, s, i, :]).then_inc(x_stat, 1)
                dve.wait_ge(x_stat, n + 2)
                dve.tensor_tensor(xsum[:, s, two], xstat[:, s, two, 1], xstat[:, s, two, 4],
                                  ALU.add).then_inc(x_sum, 1)
                dve.wait_ge(x_sum, m + 1)
                dve.tensor_scalar(minus_mean[:, s, two], xsum[:, s, two], -0.5, None, ALU.mult).then_inc(x_mean, 1)
                if t == T - 2:
                    b = SLOTS * p + s
                    dve.tensor_tensor(xdiff[:, s, :], xstat[:, s, :, 1], xstat[:, s, :, 4],
                                      ALU.subtract).then_inc(x_var, 1)
                    dve.scalar_tensor_tensor(xm2[:, s, :], xstat[:, s, :, 2], D * LN_EPS, xstat[:, s, :, 5],
                                             ALU.add, ALU.add).then_inc(x_var, 1)
                    dve.wait_ge(x_var, 3 * b + 2)
                    dve.scalar_tensor_tensor(xd2[:, s, :], xdiff[:, s, :], 0.25, xdiff[:, s, :],
                                             ALU.mult, ALU.mult).then_inc(x_var, 1)
                    dve.wait_ge(x_var, 3 * b + 3)
                    dve.scalar_tensor_tensor(xve[:, s, :], xm2[:, s, :], 1.0 / D, xd2[:, s, :],
                                             ALU.mult, ALU.add).then_inc(x_ve, 1)

            def prepare_first_q(s, t):
                dve.wait_ge(x_mean, T // 2 * s + t // 2 + 1)
                for i in range(t, t + 2):
                    dve.scalar_tensor_tensor(q_prod[:, i % 2], x[:, s, i, :].unsqueeze(1).broadcast_to([P, 2, D]),
                                             minus_mean[:, s, i:i + 1], tab[:, i, 0:2, :], ALU.add,
                                             ALU.mult).then_inc(q_mul, 1)
                for i in range(t, t + 2):
                    u = T * s + i
                    dve.wait_ge(q_mul, u + 1)
                    if u >= QUERY_TILES:
                        dve.wait_ge(t_ps, u - QUERY_TILES + 1)
                    pairs = q_prod[:, i % 2].rearrange("p a (i r) -> p a i r", r=2)
                    dve.tensor_tensor(qr[:, u % QUERY_TILES, :].rearrange("p (i r) -> p i r", r=2), pairs[:, 0],
                                      pairs[:, 1, :, ::-1], ALU.add).then_inc(q_ready, 1)

            def statistics(p, e, src, todo=range(2)):
                s, d = e // 2 % SLOTS, e % 2
                m = LN_EVENTS * p + e
                n = 2 * m
                for i in todo:
                    dve.bn_stats(st[:, s, d, i, :], src(s, d, i)).then_inc(ln_st, 1)
                if 1 not in todo:
                    return
                dve.wait_ge(ln_st, n + 2)
                dve.scalar_tensor_tensor(nm2[:, s, d], st[:, s, d, :, 1], -1.0, st[:, s, d, :, 4],
                                         ALU.mult, ALU.subtract).then_inc(ln_mv, 1)
                for i in range(2):
                    dve.bn_aggr(mv[:, s, d, i, :], st[:, s, d, i, :]).then_inc(ln_mv, 1)
                dve.wait_ge(ln_mv, 3 * m + 3)
                dve.tensor_scalar(ve[:, s, d], mv[:, s, d, :, 1], LN_EPS, None, ALU.add).then_inc(ln_ve, 1)
                dve.tensor_scalar(nm[:, s, d], nm2[:, s, d], 0.5, None, ALU.mult).then_inc(ln_ve, 1)

            def x1_statistics(p, u):
                dve.wait_ge(x1_ready, UNITS * p + u + 1)
                statistics(p, ln_event(0, u // T, u % T // 2), lambda s, d, i: x1[:, s, 2 * d + i, :],
                           range(u % 2, u % 2 + 1))

            def y1_statistics(p, blk, s, halves=range(2)):
                for d in halves:
                    dve.wait_ge(y1_ps, ((BLOCKS * p + blk) * SLOTS + s) * 2 + d + 1)
                    statistics(p, ln_event(blk + 1, s, d), lambda s, d, i: bank[2 * s + d][:, i * D:(i + 1) * D])

            def evacuate_scores(p, i):
                dve.wait_ge(score_ps, 2 * UNITS * p + i + 1)
                if i >= 2:
                    dve.wait_ge(intra_ps, 2 * UNITS * p + i - 1)
                dve.tensor_tensor(sT[:, i % 2], bank[i % 2][:, :].rearrange("p (h n) -> p h n", h=HH),
                                  causal.unsqueeze(1).broadcast_to([P, HH, C]), ALU.mult).then_inc(score_ev, 1)

            def evacuate_state(p, s, k):
                n = (NC * T - 1) * (SLOTS * p + s) + k
                dve.wait_ge(state_ps, n + 1)
                u_read = T * s + (k - 3) // NC
                if k >= 3:
                    dve.wait_ge(tok_ps, UNITS * p + u_read + 1)
                quarters = [P, NF, P // PAIR_W, PAIR_W]
                dve.tensor_tensor(
                    state[:, s, (k + 1) % 4].rearrange("p f (j n) -> p f j n", n=PAIR_W),
                    bank[6 + s][:, 0:NF * PAIR_W].rearrange("p (f n) -> p f n", f=NF).unsqueeze(2).broadcast_to(quarters),
                    diag16.rearrange("p (j n) -> p j n", n=PAIR_W).unsqueeze(1).broadcast_to(quarters),
                    ALU.mult).then_inc(state_ev, 1)

            def residual_x1(p, u):
                s, t = u // T, u % T
                dve.wait_ge(tok_ps, UNITS * p + u + 1)
                dve.scalar_tensor_tensor(x1[:, s, t, :], bank[4 + u % 2][:, 0:256], row_gate[:, s, t:t + 1],
                                         x[:, s, t, :], ALU.mult, ALU.add).then_inc(x1_ready, 1)

            def evacuate_h(p):
                dve.wait_ge(h_ps, 3 * p + 3)
                dve.tensor_copy(hT[1][:, 1, :], bank[7][:, :]).then_inc(h_ev_dve, 1)

            def u_rest(p, blk, s, f=0):
                n = (BLOCKS * p + blk) * SLOTS + s
                dve.wait_ge(u_gelu, 2 * NF * n + NF + f + 1)
                dve.tensor_tensor(u_lo[:, f], u_exact[:, f], u_hi[:, f].bitcast(F32),
                                  ALU.subtract).then_inc(u_lo_ready[f], 1)

            def residual_h(p, blk, s):
                n = (BLOCKS * p + blk) * SLOTS + s
                for f in range(NF):
                    dve.wait_ge(y2_ps, NF * n + f + 1)
                    dve.scalar_tensor_tensor(hT[s][:, f, :], bank[2 * s + f][:, :], vec[:, 2, blk, f:f + 1],
                                             hT[s][:, f, :], ALU.add, ALU.add).then_inc(h_res, 1)

            def output(p, s):
                for d in range(2):
                    dve.wait_ge(o_ps, (SLOTS * p + s) * 2 + d + 1)
                    dve.scalar_tensor_tensor(zn[:, s, 2 * d:2 * d + 2, :].rearrange("p t d -> p (t d)"),
                                             bank[4 + 2 * s + d][:, :], tanh_gate[:, 1:2],
                                             x1[:, s, 2 * d:2 * d + 2, :].rearrange("p t d -> p (t d)"),
                                             ALU.mult, ALU.add).then_inc(o_ev, 1)

            def pair(p, more):
                dve.wait_ge(rg_ready, SLOTS * (p + 1))
                for i in range(2 * UNITS):
                    u, f = i // 2, i % 2
                    evacuate_scores(p, i)
                    if i >= 1 and (i - 1) % (NC * T) < NC * T - 1:
                        evacuate_state(p, (i - 1) // (NC * T), (i - 1) % (NC * T))
                    if f == 1 and u >= 1:
                        residual_x1(p, u - 1)
                        x1_statistics(p, u - 1)
                if more:
                    x_statistics(p + 1, 0, 0)
                residual_x1(p, UNITS - 1)
                x1_statistics(p, UNITS - 1)
                y1_statistics(p, 0, 0)
                evacuate_h(p)
                if more:
                    x_statistics(p + 1, 0, 2)
                for blk in range(BLOCKS):
                    for s in range(SLOTS):
                        if blk + s < BLOCKS:
                            y1_statistics(p, blk + s, 1 - s, range(0, 1))
                            u_rest(p, blk, s)
                            y1_statistics(p, blk + s, 1 - s, range(1, 2))
                        else:
                            for f in range(NF):
                                u_rest(p, blk, s, f)
                            output(p, 0)
                        residual_h(p, blk, s)
                        if more and (blk, s) in ((0, 0), (0, 1)):
                            x_statistics(p + 1, 1, 2 * s)
                output(p, 1)

            dve.memset(bias_rows[:, :, :].rearrange("p b d -> p (b d)"), 0.0).then_inc(bias_set, 1)
            for s in range(SLOTS):
                for t in range(0, T, 2):
                    dve.wait_ge(tab_in[t // 2], 16)
                    x_statistics(0, s, t)
                    prepare_first_q(s, t)
            for k in range(NF):
                dve.wait_ge(scale_in[k], 16)
                for l in range(LAYERS):
                    dve.wait_ge(w_deq, l + 1)
                    dve.tensor_tensor(weight(l)[:, k], weight(l)[:, k], w_scale[:, k, l * D:(l + 1) * D],
                                      ALU.mult).then_inc(w_scaled, 1)
            for l in range(LAYERS):
                dve.wait_ge(w_scaled, LAYERS + l + 1)
                dve.wait_ge(lora_ps, l + 1)
                dve.tensor_tensor(weight(l).rearrange("p k o -> p (k o)"), bank[l][:, :],
                                  weight(l).rearrange("p k o -> p (k o)"), ALU.add).then_inc(w_ready, 1)
            dve.wait_ge(gate_tanh, 1)
            dve.wait_ge(const_in, 16)
            dve.wait_ge(vec_in, 16)
            with dve.Fori(0, PAIRS - 1) as p:
                pair(p, True)
            pair(PAIRS - 1, False)

        @block.tensor
        def _(pe):
            def transpose_qk(p, u, dst):
                s, t = u // T, u % T
                pe.wait_ge(q_ready, UNITS * p + u + 1)
                pe.wait_ge(k_ready, UNITS * p + u + 1)
                for a, src in enumerate((qr[:, u % QUERY_TILES], kr[:, s, t])):
                    for f in range(NF):
                        col = (a * NF + f) * P
                        last = pe.transpose(dst[:, col:col + P], src[:, f * P:(f + 1) * P], ident)
                last.then_inc(t_ps, 1)

            def scores(p, i):
                u, f = i // 2, i % 2
                s, t = u // T, u % T
                if u % T == 0 and f == 0:
                    pe.wait_ge(wide_in[s], 16 * HH * (p + 1))
                    pe.wait_ge(t_ev, 2 * UNITS * (p + 1))
                    pe.wait_ge(v_ready, NC * (SLOTS * p + s + 1))
                    pe.wait_ge(ctx_in[s], 16 * (p + 1))
                if i >= 2:
                    pe.wait_ge(score_ev, 2 * UNITS * p + i - 1)
                for c in range(NC):
                    cols = slice(t * P + c * C, t * P + (c + 1) * C)
                    last = pe.matmul(bank[i % 2][c * C:(c + 1) * C, :], kT[:, s, f, cols], q_wide[:, s, f, :, cols],
                                     start=True, stop=True)
                last.then_inc(score_ps, 1)

            def update_state(p, s, k):
                t, c = k // NC, k % NC
                n = (NC * T - 1) * (SLOTS * p + s) + k
                if k >= 1:
                    pe.wait_ge(state_ev, n)
                elif s == 0:
                    pe.wait_ge(t_ev, 2 * UNITS * (p + 1))
                for f in range(NF):
                    for j in range(P // PAIR_W):
                        heads = slice(HH * f + 2 * j, HH * f + 2 * j + 2)
                        cols = slice(PAIR_W * j, PAIR_W * (j + 1))
                        last = pe.matmul(bank[6 + s][cols, f * PAIR_W:(f + 1) * PAIR_W],
                                         kr[:, s, t, f * P + PAIR_W * j:f * P + PAIR_W * (j + 1)],
                                         v_chunk[:, s, t, heads, c, :],
                                         start=(k == 0 and f == 0), stop=(k == NC * T - 2), skip_group_check=True)
                last.then_inc(state_ps, 1)

            def intra_chunk(p, i):
                u, f = i // 2, i % 2
                s, t = u // T, u % T
                pe.wait_ge(score_ev, 2 * UNITS * p + i + 1)
                if f == 0 and u >= 2:
                    pe.wait_ge(intra_ev, UNITS * p + u - 1)
                for h in range(HH):
                    head = HH * f + h
                    j, g = head % 4, head // 4
                    last = pe.matmul(bank[2 + u % 2][32 * j:32 * (j + 1), g * C:(g + 1) * C],
                                     v_chunk[:, s, t, head].rearrange("p c e -> p (c e)"), sT[:, i % 2, h, :],
                                     start=True, stop=True)
                last.then_inc(intra_ps, 1)

            def to_tokens(p, u):
                s, t = u // T, u % T
                pe.wait_ge(intra_ev, UNITS * p + u + 1)
                if u >= 2:
                    pe.wait_ge(x1_ready, UNITS * p + u - 1)
                k = min(NC * t, NC * T - 2)
                pe.wait_ge(state_ev, (NC * T - 1) * (SLOTS * p + s) + k + 1)
                out = bank[4 + u % 2]
                for c in range(NC):
                    chunk = NC * t + c
                    rows = slice(c * C, (c + 1) * C)
                    first = True
                    if chunk > 0:
                        for f in range(NF):
                            pe.matmul(out[rows, f * P:(f + 1) * P], qT[:, s, f, chunk * C:(chunk + 1) * C],
                                      state[:, s, chunk % 4, f, :], start=first, stop=False, skip_group_check=True)
                            first = False
                    for g in range(HEADS // 4):
                        last = pe.matmul(out[rows, g * C:(g + 1) * C], intra[:, u % 2, g, :], pick[:, c, :],
                                         start=first, stop=True, skip_group_check=True)
                        first = False
                last.then_inc(tok_ps, 1)

            def transpose_half(dst, s, f):
                for t in range(T):
                    last = pe.transpose(dst[:, t * P:(t + 1) * P], zn[:, s, t, f * P:(f + 1) * P], ident)
                return last

            def h_to_features(p):
                pe.wait_ge(zn_ready, 2 * LN_EVENTS * p + 2 * ln_event(0, 1, 1) + 2)
                pe.wait_ge(h_ev_act, 3 * p + NF)
                for f in range(NF):
                    last = transpose_half(bank[6 + f], 1, f)
                last.then_inc(h_ps, 1)

            def h_half_to_features(p, f):
                if f == 0:
                    pe.wait_ge(zn_ready, 2 * LN_EVENTS * p + 2 * ln_event(0, 0, 1) + 2)
                else:
                    pe.wait_ge(h_ev_act, 3 * p + f)
                transpose_half(bank[6], 0, f).then_inc(h_ps, 1)

            def linear1_head(p, blk, s, t):
                n = (BLOCKS * p + blk) * SLOTS + s
                if t == 0 and blk == 0:
                    pe.wait_ge(h_ev_act, 3 * p + NF + s)
                    if s == 1:
                        pe.wait_ge(h_ev_dve, p + 1)
                elif blk > 0 and t % 2 == 0:
                    pe.wait_ge(h_res, NF * (n - SLOTS) + 1 + t // 2)
                if blk == 0 and s == 0 and t == 0:
                    pe.wait_ge(bias_set, 4)
                    pe.wait_ge(ones_set, 1)
                out = bank[2 * s + t // 2][:, (t % 2) * D:(t % 2 + 1) * D]
                pe.matmul(out, ones[:, :], bias_rows[:, blk, :], start=(t % 2 == 0), stop=False, skip_group_check=True)
                pe.matmul(out, hT[s][:, 0, t * P:(t + 1) * P], w1[:, blk, 0, :], start=False, stop=False,
                          skip_group_check=True)

            def linear1_tail(p, blk, s, t):
                n = (BLOCKS * p + blk) * SLOTS + s
                if blk > 0 and t == 0:
                    pe.wait_ge(h_res, NF * (n - SLOTS) + 2)
                out = bank[2 * s + t // 2][:, (t % 2) * D:(t % 2 + 1) * D]
                last = pe.matmul(out, hT[s][:, 1, t * P:(t + 1) * P], w1[:, blk, 1, :], start=False, stop=True,
                                 skip_group_check=True)
                if t % 2 == 1:
                    last.then_inc(y1_ps, 1)

            def linear1(p, blk, s, tiles=range(T)):
                for t in tiles:
                    linear1_head(p, blk, s, t)
                    linear1_tail(p, blk, s, t)

            def z_to_features(p, blk, s, d, more):
                pe.wait_ge(zn_ready, 2 * LN_EVENTS * p + 2 * ln_event(blk + 1, s, d) + 2)
                e = SLOTS * blk + s
                if more and d == 0 and e in (3, 4):
                    pe.wait_ge(t_ev, 2 * UNITS * (p + 1) + 4 * (e - 3) + 4)
                for f in range(NF):
                    for t in range(2 * d, 2 * d + 2):
                        last = pe.transpose(bank[4 + 2 * s + f][:, t * P:(t + 1) * P],
                                            zn[:, s, t, f * P:(f + 1) * P], ident)
                if d == 1:
                    last.then_inc(z_ps, 1)

            def linear2(p, blk, s):
                n = (BLOCKS * p + blk) * SLOTS + s
                if blk == 0 and s == 0:
                    pe.wait_ge(w2_rest, BLOCKS)
                pe.wait_ge(u_gelu, 2 * NF * n + NF)
                for f in range(NF):
                    for i, (w, k) in enumerate((w, k) for k in range(NF) for w in (w2_hi, w2_lo)):
                        pe.matmul(bank[2 * s + f][:, :], w[:, blk, k, f * P:(f + 1) * P], u_hi[:, k, :],
                                  start=(i == 0), stop=False)
                for f in range(NF):
                    for k in range(NF):
                        if f == 0:
                            pe.wait_ge(u_lo_ready[k], n + 1)
                        last = pe.matmul(bank[2 * s + f][:, :], w2_hi[:, blk, k, f * P:(f + 1) * P], u_lo[:, k, :],
                                         start=False, stop=(k == NF - 1))
                    last.then_inc(y2_ps, 1)

            def h_to_tokens(p, s):
                n = (BLOCKS * p + BLOCKS - 1) * SLOTS + s
                for f in range(NF):
                    pe.wait_ge(h_res, NF * n + f + 1)
                    for t in range(T):
                        col = (t % 2) * D + f * P
                        last = pe.transpose(bank[4 + 2 * s + t // 2][:, col:col + P],
                                            hT[s][:, f, t * P:(t + 1) * P], ident)
                        if f == NF - 1 and t % 2 == 1:
                            last.then_inc(o_ps, 1)

            def transpose_next(p, s, free, turn):
                for j in range(2):
                    u = T * s + 2 * turn + j
                    if s == 1 and turn == 1:
                        pe.wait_ge(t_ev, 2 * UNITS * (p + 1) + 2 * (u - 2) + 2)
                    transpose_qk(p + 1, u, bank[free + j])

            def pair(p, more):
                for i in range(2 * UNITS):
                    u, f = i // 2, i % 2
                    scores(p, i)
                    if i >= 1:
                        intra_chunk(p, i - 1)
                        if (i - 1) % (NC * T) < NC * T - 1:
                            update_state(p, (i - 1) // (NC * T), (i - 1) % (NC * T))
                    if i == 2 * (T + 2):
                        h_half_to_features(p, 0)
                    if i == 2 * UNITS - 1:
                        h_half_to_features(p, 1)
                        intra_chunk(p, i)
                    if f == 1 and u >= 1:
                        to_tokens(p, u - 1)
                to_tokens(p, UNITS - 1)

                linear1(p, 0, 0)
                h_to_features(p)
                for blk in range(BLOCKS):
                    for s in range(SLOTS):
                        other = blk + s < BLOCKS
                        z_to_features(p, blk, s, 0, more)
                        for t in range(2) if other else []:
                            linear1_head(p, blk + s, 1 - s, t)
                        z_to_features(p, blk, s, 1, more)
                        if other:
                            for t in range(2):
                                linear1_tail(p, blk + s, 1 - s, t)
                            linear1(p, blk + s, 1 - s, range(2, T))
                        else:
                            h_to_tokens(p, 0)
                            if more:
                                transpose_next(p, 1, 0, 0)
                        linear2(p, blk, s)
                        e = SLOTS * blk + s
                        if more and e in (1, 2):
                            transpose_next(p, 0, 4 + 2 * s, e - 1)
                if more:
                    transpose_next(p, 1, 0, 1)
                h_to_tokens(p, 1)

            def lora_product(l):
                rows = slice(RANK * (l % LORA_ROWS), RANK * (l % LORA_ROWS + 1))
                for k in range(NF):
                    last = pe.matmul(bank[l][:, k * D:(k + 1) * D], la[rows, l // LORA_ROWS, k * P:(k + 1) * P],
                                     lbt[rows, l // LORA_ROWS, :], start=True, stop=True)
                last.then_inc(lora_ps, 1)

            pe.wait_ge(const_in, 16)
            pe.wait_ge(lora_in, 32)
            for u in range(UNITS):
                if u >= 2:
                    pe.wait_ge(t_ev, 2 * u - 2)
                transpose_qk(0, u, bank[6 + u % 2])
                if u == 1 or u == 3:
                    for l in range(LAYERS // 2 * (u // 2), LAYERS // 2 * (u // 2 + 1)):
                        lora_product(l)
            pe.wait_ge(w_ready, LAYERS)
            with pe.Fori(0, PAIRS - 1) as p:
                pair(p, True)
            pair(PAIRS - 1, False)


def constants():
    f = np.float32
    lin = np.linspace(np.log(1.0 / 32.0), np.log(1.0 / 512.0), HEADS).astype(f)
    gamma = (f(1.0) - np.exp(lin)).astype(f).astype(np.float64)
    pos = np.arange(S, dtype=f)
    base = ((np.arange(0, HD, 2, dtype=f) + f(0.4 * HD)) / f(1.4 * HD)).astype(np.float64)
    scale = base[None, :] ** (pos.astype(np.float64) / 512.0)[:, None]
    inv_freq = (1.0 / 10000.0 ** (np.arange(HD // 2, dtype=f) / f(HD // 2))).astype(f)
    angle = (pos[:, None] * inv_freq[None, :]).astype(f).astype(np.float64)
    decay = gamma[None, :] ** (pos.astype(np.float64) - S // 2)[:, None]

    def table(trig, sign, scl, dec):
        return dec[:, :, None, None] * (trig * scl)[:, None, :, None] * np.array(sign)[None, None, None, :]

    tabs = [table(np.cos(angle), [1, 1], scale, decay), table(np.sin(angle), [1, -1], scale, decay),
            table(np.cos(angle), [1, 1], 1 / scale, 1 / decay), table(np.sin(angle), [1, -1], 1 / scale, 1 / decay)]
    tab = np.stack([a.reshape(T, P, D) for a in tabs], axis=2).transpose(1, 0, 2, 3)
    i = np.arange(P)
    const = np.zeros((P, C_END), f)
    const[:, C_ID:C_ID + P] = np.eye(P)
    const[:, C_DIAG:C_DIAG + P] = i[:, None] // HD == i[None, :] // HD
    for c in range(NC):
        for j in range(4):
            for e in range(HD):
                const[32 * j + HD * c + e, C_PICK + c * C + HD * j + e] = 1
    const[:, C_CAUSAL:C_CAUSAL + C] = np.arange(C)[None, :] >= i[:, None] % C
    return const, np.ascontiguousarray(tab.astype(f))


def kernel(x, ctx_1024, g_xattn, g_ffn, L0_ffn_qweights, L0_ffn_scales, L0_ffn_biases, L0_ffn_lora_a, L0_ffn_lora_b,
           L0_ffn_ln_gamma, L0_ffn_ln_beta):
    import concourse.bacc as bacc
    from concourse.bass_utils import run_bass_kernel_spmd

    def c(a):
        return np.ascontiguousarray(a)

    def rows_below(a):
        return c(a.reshape(-1, LORA_ROWS, RANK, D).transpose(1, 2, 0, 3).reshape(LORA_ROWS * RANK, -1, D))

    const, tab = constants()
    q, biases = np.asarray(L0_ffn_qweights), np.asarray(L0_ffn_biases)
    vec = np.stack([np.asarray(L0_ffn_ln_gamma), np.asarray(L0_ffn_ln_beta), biases[1::2]])
    arrays = {
        "x": c(x), "ctx": c(ctx_1024),
        "gates": c(np.concatenate([np.asarray(g_xattn), np.asarray(g_ffn)])),
        "qweights": c(q.transpose(2, 0, 1).reshape(NF, P, LAYERS, D).transpose(1, 2, 0, 3).reshape(P, LAYERS * NF, D)),
        "scales": c(np.asarray(L0_ffn_scales).transpose(2, 0, 1).reshape(D // GROUP, LAYERS * D)),
        "bias1": c(biases[0::2]),
        "lora_a": rows_below(np.asarray(L0_ffn_lora_a)),
        "lora_bt": rows_below(np.asarray(L0_ffn_lora_b).transpose(0, 2, 1)),
        "vectors": c(vec.reshape(3, BLOCKS, NF, P).transpose(3, 0, 1, 2)),
        "const": const, "tables": tab,
    }
    nc = bacc.Bacc("TRN2", target_bir_lowering=False, num_devices=1)
    args = [nc.dram_tensor(f"in_{k}", a.shape, mybir.dt.from_np(a.dtype), kind="ExternalInput").ap()
            for k, a in arrays.items()]
    out = nc.dram_tensor("out", (B, S, D), F32, kind="ExternalOutput").ap()
    build(nc, *args, out)
    r = run_bass_kernel_spmd(nc, [{f"in_{k}": a for k, a in arrays.items()}], core_ids=[0])
    return r.results[0]["out"]
```
